# Optimizing a Trainium2 kernel written in Bass

```python
import numpy as np
import jax
import jax.numpy as jnp

def _softmax(x, axis=-1):
    return jax.nn.softmax(x, axis=axis)

def _gelu(x):
    return jax.nn.gelu(x, approximate=True)

def _silu(x):
    return jax.nn.silu(x)

def _sigmoid(x):
    return jax.nn.sigmoid(x)

def _layernorm(x, axis=-1, eps=1e-05):
    m = jnp.mean(x, axis=axis, keepdims=True)
    v = jnp.var(x, axis=axis, keepdims=True)
    return (x - m) / jnp.sqrt(v + eps)

def _scatter_add(tgt, idx, src, axis=0):
    return tgt.at[idx].add(src)

def _segment_sum(src, seg, n):
    return jax.ops.segment_sum(src, seg, n)
kernel_name = 'mk_xattn_ffn_d1_seqx_r8_356559'

def setup_inputs(seed: int=0):
    np.random.seed(seed)
    _w = jnp.asarray

    def _rec_inputs():
        import jax
        import jax.numpy as jnp
        _rk = jax.random.key(seed)
        x = -0.000125 + 0.9999 * jax.random.normal(jax.random.fold_in(_rk, 1), (4, 256, 256), jnp.float32)
        _lenS = 256 - jax.random.randint(jax.random.fold_in(_rk, 7), (4,), 0, max(1, 256 // 4) + 1, jnp.int32)
        _lenS2 = 256 - jax.random.randint(jax.random.fold_in(_rk, 8), (4,), 0, max(1, 256 // 4) + 1, jnp.int32)
        _ctx_2048P = jax.random.normal(jax.random.fold_in(_rk, 11), (4, 16, 256), jnp.float32)
        _ctx_2048c = jax.random.dirichlet(jax.random.fold_in(_rk, 511), 0.3 * jnp.ones((16,), jnp.float32), (4, 256))
        _ctx_2048t = jnp.einsum('bsk,bkd->bsd', _ctx_2048c, _ctx_2048P)
        _ctx_2048t = _ctx_2048t * jax.lax.rsqrt(jnp.mean(jnp.square(_ctx_2048t)) + 1e-12) * 0.953939
        ctx_2048 = 4.13588e-05 + 0.999923 * (_ctx_2048t + 0.3 * jax.random.normal(jax.random.fold_in(_rk, 611), (4, 256, 256), jnp.float32))
        return (x, ctx_2048)
    x, ctx_2048 = _rec_inputs()

    def _L0_xattn_setup():
        import jax, jax.numpy as jnp
        import numpy as np
        D_MODEL = 256
        NUM_HEADS = 16
        HEAD_DIM = D_MODEL // NUM_HEADS
        key = jax.random.key(seed)
        ks = jax.random.split(key, 10)
        B, S, T = (4, 512, 128)
        s = 1.0 / np.sqrt(D_MODEL)
        inp = {'query': jax.random.normal(ks[0], (B, S, D_MODEL), jnp.float32), 'key_value': jax.random.normal(ks[1], (B, T, D_MODEL), jnp.float32), 'Wq': jax.random.normal(ks[2], (D_MODEL, D_MODEL), jnp.float32) * s, 'bq': jnp.zeros((D_MODEL,), jnp.float32), 'Wk': jax.random.normal(ks[3], (D_MODEL, D_MODEL), jnp.float32) * s, 'bk': jnp.zeros((D_MODEL,), jnp.float32), 'Wv': jax.random.normal(ks[4], (D_MODEL, D_MODEL), jnp.float32) * s, 'bv': jnp.zeros((D_MODEL,), jnp.float32), 'Wo': jax.random.normal(ks[5], (D_MODEL, D_MODEL), jnp.float32) * s, 'bo': jnp.zeros((D_MODEL,), jnp.float32)}
        return inp
    _L0_xattn_all = _L0_xattn_setup()
    _L0_xattn_in = {k: v for k, v in _L0_xattn_all.items() if k in ('Wq', 'bq', 'Wk', 'bk', 'Wv', 'bv', 'Wo', 'bo')}
    del _L0_xattn_all

    def _L0_ffn_setup():
        import jax, jax.numpy as jnp
        import numpy as np
        B, S, H = (4, 256, 256)
        E = 8
        F = H // E
        TOPK = 2
        LORA_R = 16
        LORA_SCALE = 1.0
        key = jax.random.key(seed)
        ks = jax.random.split(key, 7)
        x = jax.random.normal(ks[0], (B, S, H), dtype=jnp.float32)
        G = jax.random.normal(ks[1], (H, E), dtype=jnp.float32)
        gate_w = jax.random.normal(ks[2], (E, F, H), dtype=jnp.float32) * np.float32(np.sqrt(2.0 / H))
        up_w = jax.random.normal(ks[3], (E, F, H), dtype=jnp.float32) * np.float32(np.sqrt(2.0 / H))
        down_w = jax.random.normal(ks[4], (E, H, F), dtype=jnp.float32) * np.float32(np.sqrt(2.0 / F))
        lora_A = jax.random.normal(ks[5], (E, LORA_R, H), dtype=jnp.float32) * np.float32(np.sqrt(2.0 / H))
        lora_B = jax.random.normal(ks[6], (E, H, LORA_R), dtype=jnp.float32) * np.float32(np.sqrt(2.0 / LORA_R))
        return {'x': x, 'G': G, 'gate_w': gate_w, 'up_w': up_w, 'down_w': down_w, 'lora_A': lora_A, 'lora_B': lora_B}
    _L0_ffn_all = _L0_ffn_setup()
    _L0_ffn_in = {k: v for k, v in _L0_ffn_all.items() if k in ('G', 'gate_w', 'up_w', 'down_w', 'lora_A', 'lora_B')}
    del _L0_ffn_all
    return {'x': x, 'ctx_2048': ctx_2048, 'L0_xattn_Wq': _L0_xattn_in['Wq'], 'L0_xattn_bq': _L0_xattn_in['bq'], 'L0_xattn_Wk': _L0_xattn_in['Wk'], 'L0_xattn_bk': _L0_xattn_in['bk'], 'L0_xattn_Wv': _L0_xattn_in['Wv'], 'L0_xattn_bv': _L0_xattn_in['bv'], 'L0_xattn_Wo': _L0_xattn_in['Wo'], 'L0_xattn_bo': _L0_xattn_in['bo'], 'L0_ffn_G': _L0_ffn_in['G'], 'L0_ffn_gate_w': _L0_ffn_in['gate_w'], 'L0_ffn_up_w': _L0_ffn_in['up_w'], 'L0_ffn_down_w': _L0_ffn_in['down_w'], 'L0_ffn_lora_A': _L0_ffn_in['lora_A'], 'L0_ffn_lora_B': _L0_ffn_in['lora_B']}

def reference(x, ctx_2048, L0_xattn_Wq, L0_xattn_bq, L0_xattn_Wk, L0_xattn_bk, L0_xattn_Wv, L0_xattn_bv, L0_xattn_Wo, L0_xattn_bo, L0_ffn_G, L0_ffn_gate_w, L0_ffn_up_w, L0_ffn_down_w, L0_ffn_lora_A, L0_ffn_lora_B):
    import jax
    import jax.numpy as jnp

    def _L0_xattn_ref(query, key_value, Wq, bq, Wk, bk, Wv, bv, Wo, bo):
        import jax, jax.numpy as jnp
        import numpy as np
        D_MODEL = 256
        NUM_HEADS = 16
        HEAD_DIM = D_MODEL // NUM_HEADS
        B, S, _ = query.shape
        T = key_value.shape[1]
        Q = query @ Wq.T + bq
        K = key_value @ Wk.T + bk
        V = key_value @ Wv.T + bv
        Q = Q.reshape(B, S, NUM_HEADS, HEAD_DIM).transpose(0, 2, 1, 3)
        K = K.reshape(B, T, NUM_HEADS, HEAD_DIM).transpose(0, 2, 1, 3)
        V = V.reshape(B, T, NUM_HEADS, HEAD_DIM).transpose(0, 2, 1, 3)
        scale = 1.0 / np.sqrt(HEAD_DIM).astype(np.float32)
        scores = jnp.einsum('bhsd,bhtd->bhst', Q, K) * scale
        attn = jax.nn.softmax(scores, axis=-1)
        ctx = jnp.einsum('bhst,bhtd->bhsd', attn, V)
        ctx = ctx.transpose(0, 2, 1, 3).reshape(B, S, D_MODEL)
        return ctx @ Wo.T + bo

    def _L0_ffn_ref(x, G, gate_w, up_w, down_w, lora_A, lora_B):
        import jax, jax.numpy as jnp
        import numpy as np
        B, S, H = (4, 256, 256)
        E = 8
        F = H // E
        TOPK = 2
        LORA_R = 16
        LORA_SCALE = 1.0
        scores = jax.nn.softmax(jnp.einsum('bsh,he->bse', x, G), axis=-1)
        value, indices = jax.lax.top_k(scores, TOPK)
        onehot = jax.nn.one_hot(indices, E, dtype=value.dtype)
        w = jnp.einsum('bsk,bske->bse', value, onehot)
        gate = jax.nn.silu(jnp.einsum('bsh,efh->bsef', x, gate_w))
        up = jnp.einsum('bsh,efh->bsef', x, up_w)
        gated = gate * up
        out = jnp.einsum('bsef,bse,ehf->bsh', gated, w, down_w)
        lr = jnp.einsum('bsh,erh->bser', x, lora_A)
        out = out + LORA_SCALE * jnp.einsum('bser,bse,ehr->bsh', lr, w, lora_B)
        return out
    x = x + _L0_xattn_ref(_layernorm(x, axis=-1), ctx_2048, L0_xattn_Wq, L0_xattn_bq, L0_xattn_Wk, L0_xattn_bk, L0_xattn_Wv, L0_xattn_bv, L0_xattn_Wo, L0_xattn_bo)
    x = x + _L0_ffn_ref(_layernorm(x, axis=-1), L0_ffn_G, L0_ffn_gate_w, L0_ffn_up_w, L0_ffn_down_w, L0_ffn_lora_A, L0_ffn_lora_B)
    return x

_drawn_inputs = setup_inputs


def setup_inputs(seed=0):
    import zlib

    import numpy as np

    out = dict(_drawn_inputs(seed))
    spreads = {'L0_xattn_bq': (0.0, 0.1),
     'L0_xattn_bk': (0.0, 0.1),
     'L0_xattn_bv': (0.0, 0.1),
     'L0_xattn_bo': (0.0, 0.1)}
    factors = {}
    for name, (base, spread) in spreads.items():
        noise = np.random.default_rng([zlib.crc32(name.encode()), seed]).standard_normal(out[name].shape)
        drawn = base * np.exp(spread * noise) if base else spread * noise
        out[name] = jnp.asarray(drawn.astype(out[name].dtype))
    for name, factor in factors.items():
        out[name] = (out[name] * factor).astype(out[name].dtype)
    return out
```

```python
from contextlib import ExitStack

import concourse.bass as bass
from concourse import mybir

F32 = mybir.dt.float32
F32R = mybir.dt.float32r
ALU = mybir.AluOpType
ACT = mybir.ActivationFunctionType
AX = mybir.AxisListType

P = 128
B, S, T, D = 4, 256, 256, 256
HEADS = 16
HD = D // HEADS
PAIRS = HEADS // 2
E, F, R = 8, 32, 16
EF, ER = E * F, E * R
KT = D // P
ST = S // P
TT = T // P
QUAD = 32
GROUPS = HEADS // 4
BLK = S // QUAD
EPS = 1e-5
SCALE = HD ** -0.5
NSTACK = 3
NPROB = 8
NWORK = 3
ROWS = 3 * QUAD
MROW = ROWS + HEADS

PREP = ["ln1", "xT", "k", "q", "v"]
POST = ["o", "ln2", "x2T", "logits", "gate", "lora", "up", "route", "wsel", "wsel2", "down"]
WORK_STAGES = {"xT", "k", "q", "v", "mrow", "o", "x2T", "logits", "gate", "lora", "up", "wsel",
               "wsel2", "down"}


def plan():
    order = [(s, 0, 0) for s in PREP]
    post_at = {"o": 0, "ln2": 0, "x2T": 2, "logits": 2, "gate": 3, "lora": 4, "up": 4, "route": 5,
               "wsel": 7, "wsel2": 7, "down": 8}
    prep_at = {"ln1": 8, "xT": 10, "k": 11, "q": 12, "v": 13}
    for k in range(-1, B + 1):
        for step in range(HEADS):
            if k + 1 < B and step < 12:
                for h in range(4 * step // 3, 4 * (step + 1) // 3):
                    order.append(("max", k + 1, h))
            if k + 1 < B and step == 12:
                order.append(("mrow", k + 1, 0))
            if 0 <= k < B:
                order.append(("attn", k, step))
                if step % 4 == 1 and step > 1:
                    order.append(("pv", k, step // 4 - 1))
            if 0 <= k - 1 < B:
                order += [(s, k - 1, 0) for s in POST if post_at[s] == step]
            if k + 2 < B:
                order += [(s, k + 2, 0) for s in PREP if prep_at[s] - 6 * (k < 0) == step]
        if 0 <= k < B:
            order.append(("pv", k, GROUPS - 1))
    return order


def xattn_moe_kernel(nc, x, ctxT, wattn, wffn, woT, wdown, loraB, bq, bk, bv, bo, out):
    ORDER = plan()
    WORK, used = {}, 0
    for name, b, _ in ORDER:
        if name in WORK_STAGES:
            WORK[name, b] = (used % NWORK, used // NWORK)
            used += 1

    with ExitStack() as ctx:
        def sb(name, shape, dt=F32):
            return ctx.enter_context(nc.sbuf_tensor(name, shape, dt))

        def sem(name):
            return ctx.enter_context(nc.semaphore(name))

        s_bank = [ctx.enter_context(nc.psum_tensor(f"s_bank{i}", [P, ST, T], F32)) for i in range(2)]
        t_bank = [ctx.enter_context(nc.psum_tensor(f"t_bank{i}", [P, TT, S], F32)) for i in range(2)]
        u_bank = ctx.enter_context(nc.psum_tensor("u_bank", [P, 2, S], F32))
        work = [ctx.enter_context(nc.psum_tensor(f"work{i}", [P, 2, S], F32)) for i in range(NWORK)]

        WA, WF = 3 * D, 2 * EF + ER + QUAD
        wa_hi, wa_lo = sb("wa_hi", [P, KT, WA], F32R), sb("wa_lo", [P, KT, WA], F32R)
        wf_hi, wf_lo = sb("wf_hi", [P, KT, WF], F32R), sb("wf_lo", [P, KT, WF], F32R)
        wo = sb("wo", [P, KT, D])
        wd = sb("wd", [P, EF // P, D])
        lb = sb("lb", [P, D])
        bq_sb, bk_sb = sb("bq_sb", [P, KT]), sb("bk_sb", [P, KT])
        bv_sb, bo_sb = sb("bv_sb", [P, D]), sb("bo_sb", [P, D])
        ident = sb("ident", [P, P])
        sel_f = sb("sel_f", [QUAD, 3, P])
        sel = sb("sel", [QUAD, 3, P], F32R)
        pref = sb("pref", [QUAD, BLK, E])
        mhalf = sb("mhalf", [P, ST])

        xs = sb("xs", [P, B, ST, D])
        xo = sb("xo", [P, 2, ST, D])
        cT = sb("cT", [P, 2, KT, T])
        cT_hi, cT_lo = sb("cT_hi", [P, KT, T], F32R), sb("cT_lo", [P, KT, T], F32R)
        stats = sb("stats", [P, 2, B, ST, 6])
        mv = sb("mv", [P, 2, B, ST, 2])
        vare = sb("vare", [P, 2, B, ST])
        rstd = sb("rstd", [P, 2, B, ST])
        xn = sb("xn", [P, 2, ST, D])
        xT_hi, xT_lo = sb("xT_hi", [P, 2, KT, S], F32R), sb("xT_lo", [P, 2, KT, S], F32R)
        k_hi, k_lo = sb("k_hi", [P, KT, T], F32R), sb("k_lo", [P, KT, T], F32R)
        q_hi, q_lo = sb("q_hi", [P, KT, S], F32R), sb("q_lo", [P, KT, S], F32R)
        vaug = sb("vaug", [P, 3, TT, HEADS, QUAD])
        kstack = [sb(f"kstack{i}", [P, HEADS, T], F32R) for i in range(NSTACK)]
        qstack = [sb(f"qstack{i}", [P, PAIRS, S], F32R) for i in range(NSTACK)]
        rowmax = sb("rowmax", [P, 2, ST, HEADS])
        probs = sb("probs", [P, NPROB, TT, S])
        flat_probs = probs[:].rearrange("p n t s -> p (n t s)")
        wa = flat_probs[:, 0:KT * WA].rearrange("p (k o) -> p k o", k=KT)
        wf = flat_probs[:, KT * WA:KT * (WA + WF)].rearrange("p (k o) -> p k o", k=KT)
        uT = sb("uT", [P, GROUPS, BLK, QUAD])
        rden = sb("rden", [P, GROUPS, BLK])
        un = sb("un", [P, 2, BLK, 2, HD])
        attnT = sb("attnT", [P, 2, S])
        x2 = sb("x2", [P, 2, ST, D])
        logT = sb("logT", [QUAD, BLK, QUAD])
        rt = sb("rt", [QUAD, 8, BLK, E])
        r1 = sb("r1", [QUAD, 8, BLK])
        wpad = sb("wpad", [QUAD, BLK, QUAD])
        wT = sb("wT", [QUAD, S])
        wT_hi, wT_lo = sb("wT_hi", [QUAD, S], F32R), sb("wT_lo", [QUAD, S], F32R)
        th = sb("th", [P, 2, S])
        gu = sb("gu", [P, 2, S])
        gated = sb("gated", [P, 2, S])
        lr = sb("lr", [P, S])
        lrw = sb("lrw", [P, S])
        res = sb("res", [P, 2, ST, D])

        k_parts = nc.dram_tensor("k_parts", [2, 2, D, T], F32, kind="Internal").ap()
        q_parts = nc.dram_tensor("q_parts", [2, 2, D, S], F32, kind="Internal").ap()

        x_in = [sem(f"x_in{b}") for b in range(B)]
        c_in = [sem(f"c_in{b}") for b in range(B)]
        wk_in, wq_in, wv_in, wf_in = sem("wk_in"), sem("wq_in"), sem("wv_in"), sem("wf_in")
        bias_in, wo_in, wd_in = sem("bias_in"), sem("wo_in"), sem("wd_in")
        consts = sem("consts")
        kzero = sem("kzero")
        vones = sem("vones")
        wa_hi_ready, wa_lo_ready = sem("wa_hi_ready"), sem("wa_lo_ready")
        wf_ready = sem("wf_ready")
        work_ready = [sem(f"work_ready{i}") for i in range(NWORK)]
        work_free = [sem(f"work_free{i}") for i in range(NWORK)]
        moments = sem("moments")
        rstd_ready = sem("rstd_ready")
        xn_ready = sem("xn_ready")
        dve_chain = sem("dve_chain")
        pool_chain = sem("pool_chain")
        hi_ready = sem("hi_ready")
        c_ready = sem("c_ready")
        khi_ready, qhi_ready = sem("khi_ready"), sem("qhi_ready")
        k_stored, q_stored = sem("k_stored"), sem("q_stored")
        k_stacked = [sem(f"k_stacked{i}") for i in range(NSTACK)]
        q_stacked = [sem(f"q_stacked{i}") for i in range(NSTACK)]
        s_ready, max_done = sem("s_ready"), sem("max_done")
        mrow_ready = sem("mrow_ready")
        t_ready, exp_done = sem("t_ready"), sem("exp_done")
        pv_done, u_read = sem("pv_done"), sem("u_read")
        attn_ready = sem("attn_ready")
        xo_ready = sem("xo_ready")
        logits_ready, e_ready = sem("logits_ready"), sem("e_ready")
        wT_ready = sem("wT_ready")
        th_ready = sem("th_ready")
        stored = [sem(f"stored{b}") for b in range(B)]

        LN = {}
        for name, b, _ in ORDER:
            if name in ("ln1", "ln2"):
                LN[int(name == "ln2"), b] = len(LN)

        block = ctx.enter_context(nc.Block())

        @block.sync
        def _(sp):
            for k in range(KT):
                if k == 0:
                    sp.dma_start(xs[:, 0], x[0].rearrange("(t p) d -> p t d", p=P)).then_inc(x_in[0], 16)
            wview = wattn.rearrange("(k p) o -> p k o", p=P)
            sp.dma_start(wa[:, :, 0:D], wview[:, :, 0:D]).then_inc(wk_in, 16)
            sp.dma_start(wa[:, :, D:2 * D], wview[:, :, D:2 * D]).then_inc(wq_in, 16)
            sp.dma_start(wa[:, :, 2 * D:3 * D], wview[:, :, 2 * D:3 * D]).then_inc(wv_in, 16)
            sp.dma_start(xs[:, 1], x[1].rearrange("(t p) d -> p t d", p=P)).then_inc(x_in[1], 16)

            def later_loads():
                sp.dma_start(wo[:], woT).then_inc(wo_in, 16)
                sp.dma_start(wf[:, :, 0:2 * EF + ER + E], wffn.rearrange("(k p) o -> p k o", p=P)).then_inc(wf_in, 16)
                for b in range(2, B):
                    sp.dma_start(xs[:, b], x[b].rearrange("(t p) d -> p t d", p=P)).then_inc(x_in[b], 16)
                sp.dma_start(wd[:], wdown.rearrange("(k p) o -> p k o", p=P)).then_inc(wd_in, 16)
                sp.dma_start(lb[:], loraB).then_inc(wd_in, 16)

            for name, b, _ in ORDER:
                if name == "ln1" and b >= 2:
                    sp.wait_ge(c_ready, b - 1)
                    sp.dma_start(cT[:, b % 2], ctxT[b].rearrange("(k p) t -> p k t", p=P)).then_inc(c_in[b], 16)
                if name == "k":
                    sp.wait_ge(khi_ready, b + 1)
                    sp.dma_start(k_parts[b % 2, 0].rearrange("(k p) t -> p k t", p=P), k_hi[:].bitcast(F32)).then_inc(k_stored, 16)
                    bank, turn = WORK["k", b]
                    sp.wait_ge(work_free[bank], turn + 1)
                    sp.dma_start(k_parts[b % 2, 1].rearrange("(k p) t -> p k t", p=P), k_lo[:].bitcast(F32)).then_inc(k_stored, 16)
                    sp.wait_ge(k_stored, 32 * (b + 1))
                    if b < NSTACK:
                        sp.wait_ge(kzero, b + 1)
                    else:
                        sp.wait_ge(t_ready, HEADS * (b - NSTACK + 1))
                    for g, part in enumerate((0, 0, 1)):
                        for half in range(2):
                            src = k_parts[b % 2, part].rearrange("(p h d) t -> h d p t", h=2, d=HD)[half]
                            lo = QUAD * g + HD * half
                            dst = kstack[b % NSTACK][lo:lo + HD].bitcast(F32).rearrange("d (p h) t -> d h p t", h=2)[:, half]
                            sp.dma_start(dst, src).then_inc(k_stacked[b % NSTACK], 16)
                if name == "q":
                    sp.wait_ge(qhi_ready, b + 1)
                    sp.dma_start(q_parts[b % 2, 0].rearrange("(k p) t -> p k t", p=P), q_hi[:].bitcast(F32)).then_inc(q_stored, 16)
                    bank, turn = WORK["q", b]
                    sp.wait_ge(work_free[bank], turn + 1)
                    sp.dma_start(q_parts[b % 2, 1].rearrange("(k p) t -> p k t", p=P), q_lo[:].bitcast(F32)).then_inc(q_stored, 16)
                    sp.wait_ge(q_stored, 32 * (b + 1))
                    if b >= NSTACK:
                        sp.wait_ge(t_ready, HEADS * (b - NSTACK + 1))
                    for g, part in enumerate((0, 1, 0)):
                        sp.dma_start(qstack[b % NSTACK][QUAD * g:QUAD * (g + 1)].bitcast(F32),
                                     q_parts[b % 2, part].rearrange("(p r) s -> r p s", r=QUAD))\
                            .then_inc(q_stacked[b % NSTACK], 16)
                    if b == 0:
                        later_loads()
                if name == "down":
                    bank, turn = WORK["down", b]
                    sp.wait_ge(work_free[bank], turn + 1)
                    sp.dma_start(out[b].rearrange("(t p) d -> p t d", p=P), res[:, b % 2]).then_inc(stored[b], 16)
            for b in range(B):
                sp.wait_ge(stored[b], 16)

        @block.gpsimd
        def _(pool):
            chain, xo_count = [0], [0]

            def link(ins):
                chain[0] += 1
                ins.then_inc(pool_chain, 1)
                pool.wait_ge(pool_chain, chain[0])

            pool.memset(mhalf[:], -0.5).then_inc(consts, 1)
            link(pool.memset(ident[:], 0.0))
            pool.affine_select(out=ident[:], in_=ident[:], compare_op=ALU.not_equal, fill=1.0, base=0,
                               pattern=[[-1, P]], channel_multiplier=1).then_inc(consts, 1)
            pool.wait_ge(consts, 2)

            def context_parts(b):
                pool.wait_ge(c_in[b], 16)
                if b >= 1:
                    bank, turn = WORK["v", b - 1]
                    pool.wait_ge(work_ready[bank], turn + 1)
                link(pool.tensor_scalar(cT_hi[:], cT[:, b % 2], 1.0, None, ALU.mult))
                pool.tensor_tensor(cT_lo[:], cT[:, b % 2], cT_hi[:].bitcast(F32), ALU.subtract).then_inc(c_ready, 1)

            def stack_constants(i):
                z = kstack[i][:].bitcast(F32)
                link(pool.memset(z, 0.0))
                rows = kstack[i][ROWS:MROW]
                pool.affine_select(out=rows, in_=rows, compare_op=ALU.not_equal, fill=-1.0, base=0,
                                   pattern=[[-1, HEADS], [0, T]], channel_multiplier=1).then_inc(kzero, 1)
                pool.wait_ge(kzero, i + 1)

            def other_constants():
                for i in range(3):
                    pool.memset(vaug[:, i, :, :, HD:QUAD], 1.0).then_inc(vones, 1)
                link(pool.memset(sel_f[:, 0:2], 0.5))
                link(pool.memset(sel_f[:, 2], 1.0))
                for k, width in ((0, F), (1, F), (2, R)):
                    first = -width * (P // F) * k if k < 2 else 0
                    link(pool.affine_select(out=sel_f[:, k], in_=sel_f[:, k], compare_op=ALU.is_ge, fill=0.0,
                                            base=-first, pattern=[[1, P]], channel_multiplier=-width))
                    link(pool.affine_select(out=sel_f[:, k], in_=sel_f[:, k], compare_op=ALU.is_ge, fill=0.0,
                                            base=width - 1 + first, pattern=[[-1, P]], channel_multiplier=width))
                link(pool.tensor_scalar(sel[:], sel_f[:], 1.0, None, ALU.mult))
                link(pool.memset(wpad[:], 0.0))
                for e in range(E):
                    last = pool.memset(pref[:, :, e], float(E - e))
                link(last)
                link(pool.memset(wf[:, :, WF - QUAD + E:WF], 0.0))
                pool.wait_ge(wf_in, 16)
                link(pool.tensor_scalar(wf_hi[:], wf, 1.0, None, ALU.mult))
                pool.tensor_tensor(wf_lo[:], wf, wf_hi[:].bitcast(F32), ALU.subtract).then_inc(wf_ready, 1)

            for name, b, i in ORDER:
                if name in ("ln1", "ln2"):
                    w = int(name == "ln2")
                    n = LN[w, b]
                    pool.wait_ge(moments, n + 1)
                    link(pool.tensor_scalar(vare[:, w, b], mv[:, w, b, :, 1], EPS, None, ALU.add))
                    pool.tensor_tensor(rstd[:, w, b], vare[:, w, b], mhalf[:], ALU.pow).then_inc(rstd_ready, 1)
                if name == "ln1":
                    context_parts(b)
                    if b == 0:
                        stack_constants(0)
                if name == "q" and b == 0:
                    for n in range(1, NSTACK):
                        stack_constants(n)
                    other_constants()
                if name == "xT":
                    pool.wait_ge(bias_in, 64)
                    if b >= 2:
                        pool.wait_ge(moments, LN[1, b - 2] + 1)
                    for t in range(ST):
                        pool.tensor_tensor(xo[:, b % 2, t], xs[:, b, t], bo_sb[:], ALU.add).then_inc(xo_ready, 1)
                        xo_count[0] += 1
                if name == "mrow":
                    q = qstack[b % NSTACK][ROWS:MROW]
                    bank, turn = WORK["mrow", b]
                    pool.wait_ge(work_free[bank], turn + 1)
                    pool.wait_ge(xo_ready, xo_count[0])
                    for p in range(1, PAIRS):
                        pool.tensor_scalar(q[:, p], q[:, 0].bitcast(F32), 1.0, None, ALU.mult).then_inc(mrow_ready, 1)
                    pool.wait_ge(mrow_ready, (PAIRS - 1) * (b + 1))

        @block.scalar
        def _(act):
            act.dma_start(cT[:, 0], ctxT[0].rearrange("(k p) t -> p k t", p=P)).then_inc(c_in[0], 16)
            act.dma_start(bk_sb[:], bk).then_inc(bias_in, 16)
            act.dma_start(bq_sb[:], bq).then_inc(bias_in, 16)
            act.dma_start(bv_sb[:], bv.partition_broadcast(P)).then_inc(bias_in, 16)
            act.dma_start(bo_sb[:], bo.partition_broadcast(P)).then_inc(bias_in, 16)
            act.dma_start(cT[:, 1], ctxT[1].rearrange("(k p) t -> p k t", p=P)).then_inc(c_in[1], 16)
            for w_in, n in ((wk_in, 0), (wq_in, 1), (wv_in, 2)):
                act.wait_ge(w_in, 16)
                act.copy(wa_hi[:, :, n * D:(n + 1) * D], wa[:, :, n * D:(n + 1) * D]).then_inc(wa_hi_ready, 1)
            for name, b, i in ORDER:
                if (name, b) in WORK:
                    bank, turn = WORK[name, b]
                if name in ("xT", "x2T"):
                    n = LN[int(name == "x2T"), b]
                    act.wait_ge(work_ready[bank], turn + 1)
                    act.copy(xT_hi[:, int(name == "x2T")], work[bank][:]).then_inc(hi_ready, 1)
                if name in ("k", "q"):
                    dst, bias, done, kept = (k_hi, bk_sb, khi_ready, k_stored) if name == "k" else (q_hi, bq_sb, qhi_ready, q_stored)
                    act.wait_ge(work_ready[bank], turn + 1)
                    act.wait_ge(bias_in, 64)
                    if b:
                        act.wait_ge(kept, 32 * b)
                    for o in range(KT):
                        ins = act.activation(dst[:, o], work[bank][:, o], ACT.Identity, bias=bias[:, o:o + 1])
                    ins.then_inc(done, 1)
                if name == "mrow":
                    act.wait_ge(work_ready[bank], turn + 1)
                    act.copy(qstack[b % NSTACK][ROWS:MROW, 0], work[bank][0:HEADS, 0]).then_inc(work_free[bank], 1)
                if name == "attn":
                    n = HEADS * b + i
                    act.wait_ge(t_ready, n + 1)
                    if n == 0:
                        act.wait_ge(wa_lo_ready, 3)
                        act.wait_ge(wf_ready, 1)
                    if n >= NPROB:
                        act.wait_ge(pv_done, (n - NPROB) // 4 + 1)
                    act.activation(probs[:, n % NPROB], t_bank[n % 2][:], ACT.Exp, scale=SCALE).then_inc(exp_done, 1)
                if name == "route":
                    act.wait_ge(logits_ready, b + 1)
                    act.activation(rt[:, 1], rt[:, 0], ACT.Exp).then_inc(e_ready, 1)
                if name == "gate":
                    act.wait_ge(work_ready[bank], turn + 1)
                    act.activation(th[:], work[bank][:], ACT.Tanh, scale=0.5).then_inc(th_ready, 1)
                if name == "lora":
                    act.wait_ge(work_ready[bank], turn + 1)
                    act.copy(lr[:], work[bank][:, 0]).then_inc(work_free[bank], 1)

        @block.vector
        def _(dve):
            chain = [0]

            def link(ins):
                chain[0] += 1
                ins.then_inc(dve_chain, 1)
                dve.wait_ge(dve_chain, chain[0])

            def moments_of(src, w, b):
                for t in range(ST):
                    ins = dve.bn_stats(stats[:, w, b, t], src[:, t])
                link(ins)
                for t in range(ST):
                    ins = dve.bn_aggr(mv[:, w, b, t], stats[:, w, b, t])
                ins.then_inc(moments, 1)

            def normalise(src, w, b):
                n = LN[w, b]
                dve.wait_ge(rstd_ready, n + 1)
                for t in range(ST):
                    ins = dve.tensor_scalar(xn[:, w, t], src[:, t], mv[:, w, b, t, 0:1], rstd[:, w, b, t:t + 1],
                                            ALU.subtract, ALU.mult)
                ins.then_inc(xn_ready, 1)

            for name, b, i in ORDER:
                if (name, b) in WORK:
                    bank, turn = WORK[name, b]
                if name == "ln1":
                    dve.wait_ge(x_in[b], 16)
                    moments_of(xs[:, b], 0, b)
                    if b == 0:
                        for w_in, n in ((wk_in, 0), (wq_in, 1), (wv_in, 2)):
                            if n == 1:
                                normalise(xs[:, b], 0, b)
                            at = slice(n * D, (n + 1) * D)
                            dve.wait_ge(wa_hi_ready, n + 1)
                            dve.tensor_tensor(wa_lo[:, :, at], wa[:, :, at], wa_hi[:, :, at].bitcast(F32),
                                              ALU.subtract).then_inc(wa_lo_ready, 1)
                    else:
                        normalise(xs[:, b], 0, b)
                if name in ("xT", "x2T"):
                    w = int(name == "x2T")
                    dve.wait_ge(hi_ready, LN[w, b] + 1)
                    dve.tensor_tensor(xT_lo[:, w], work[bank][:], xT_hi[:, w].bitcast(F32), ALU.subtract)\
                        .then_inc(work_free[bank], 1)
                if name in ("k", "q"):
                    hi, lo, bias, up, kept = (k_hi, k_lo, bk_sb, khi_ready, k_stored) if name == "k" else \
                        (q_hi, q_lo, bq_sb, qhi_ready, q_stored)
                    dve.wait_ge(up, b + 1)
                    if b:
                        dve.wait_ge(kept, 32 * b)
                    for o in range(KT):
                        ins = dve.scalar_tensor_tensor(out=lo[:, o], in0=work[bank][:, o], scalar=bias[:, o:o + 1],
                                                       in1=hi[:, o].bitcast(F32), op0=ALU.add, op1=ALU.subtract)
                    ins.then_inc(work_free[bank], 1)
                if name == "v":
                    dve.wait_ge(work_ready[bank], turn + 1)
                    dve.wait_ge(bias_in, 64)
                    if b >= 3:
                        dve.wait_ge(pv_done, GROUPS * (b - 2))
                    for t in range(TT):
                        ins = dve.tensor_tensor(vaug[:, b % 3, t, :, 0:HD],
                                                work[bank][:, t].rearrange("p (h d) -> p h d", d=HD),
                                                bv_sb[:].rearrange("p (h d) -> p h d", d=HD), ALU.add)
                    ins.then_inc(work_free[bank], 1)
                if name == "max":
                    n = HEADS * b + i
                    dve.wait_ge(s_ready, n + 1)
                    dve.tensor_reduce(rowmax[:, b % 2, :, i], s_bank[n % 2][:], AX.X, ALU.max).then_inc(max_done, 1)
                if name == "pv":
                    n = GROUPS * b + i
                    dve.wait_ge(pv_done, n + 1)
                    link(dve.transpose(uT[:, i], u_bank[:, 0]))
                    link(dve.reciprocal(rden[:, i], uT[:, i, :, HD]))
                    ins = dve.tensor_tensor(un[:, i // 2, :, i % 2], uT[:, i, :, 0:HD],
                                            rden[:, i].unsqueeze(2).to_broadcast([P, BLK, HD]), ALU.mult)
                    ins.then_inc(u_read, 1)
                    if i % 2:
                        dve.wait_ge(u_read, n + 1)
                        if b and i == 1:
                            ob, ot = WORK["o", b - 1]
                            dve.wait_ge(work_ready[ob], ot + 1)
                        dve.transpose(attnT[:, i // 2], un[:, i // 2]).then_inc(attn_ready, 1)
                if name == "o":
                    dve.wait_ge(work_ready[bank], turn + 1)
                    dve.wait_ge(xo_ready, ST * (b + 1))
                    ins = dve.tensor_tensor(x2[:, b % 2], work[bank][:], xo[:, b % 2], ALU.add)
                    ins.then_inc(work_free[bank], 1)
                if name == "ln2":
                    ob, ot = WORK["o", b]
                    dve.wait_ge(work_free[ob], ot + 1)
                    moments_of(x2[:, b % 2], 1, b)
                    normalise(x2[:, b % 2], 1, b)
                if name == "logits":
                    dve.wait_ge(work_ready[bank], turn + 1)
                    dve.transpose(logT[:], work[bank][0:QUAD, 0]).then_inc(work_free[bank], 1)
                    dve.wait_ge(work_free[bank], turn + 1)
                    logit = logT[:, :, 0:E]
                    wide = lambda t: t.unsqueeze(2).to_broadcast([QUAD, BLK, E])
                    link(dve.tensor_reduce(r1[:, 0], logit, AX.X, ALU.max))
                    dve.tensor_tensor(rt[:, 0], logit, wide(r1[:, 0]), ALU.subtract).then_inc(logits_ready, 1)
                if name == "route":
                    wide = lambda t: t.unsqueeze(2).to_broadcast([QUAD, BLK, E])
                    dve.wait_ge(e_ready, b + 1)
                    link(dve.tensor_reduce(r1[:, 1], rt[:, 1], AX.X, ALU.add))
                    link(dve.reciprocal(r1[:, 2], r1[:, 1]))
                    link(dve.tensor_tensor(rt[:, 2], rt[:, 1], wide(r1[:, 2]), ALU.mult))
                    score = rt[:, 2]
                    left = score
                    for j in range(2):
                        best, same, key, first, pick = r1[:, 3 + 2 * j], rt[:, 3], rt[:, 4], r1[:, 4 + 2 * j], rt[:, 5 + j]
                        link(dve.tensor_reduce(best, left, AX.X, ALU.max))
                        link(dve.tensor_tensor(same, left, wide(best), ALU.is_equal))
                        link(dve.tensor_tensor(key, same, pref[:], ALU.mult))
                        link(dve.tensor_reduce(first, key, AX.X, ALU.max))
                        link(dve.tensor_tensor(pick, key, wide(first), ALU.is_equal))
                        if j == 0:
                            link(dve.scalar_tensor_tensor(out=rt[:, 7], in0=pick, scalar=-4.0, in1=score,
                                                          op0=ALU.mult, op1=ALU.add))
                            left = rt[:, 7]
                    link(dve.tensor_tensor(rt[:, 3], rt[:, 5], rt[:, 6], ALU.add))
                    link(dve.tensor_tensor(wpad[:, :, 0:E], score, rt[:, 3], ALU.mult))
                    link(dve.transpose(wT[:], wpad[:]))
                    link(dve.tensor_copy(wT_hi[:], wT[:]))
                    dve.tensor_tensor(wT_lo[:], wT[:], wT_hi[:].bitcast(F32), ALU.subtract).then_inc(wT_ready, 1)
                if name == "gate":
                    dve.wait_ge(th_ready, b + 1)
                    dve.scalar_tensor_tensor(out=gu[:], in0=th[:], scalar=1.0, in1=work[bank][:], op0=ALU.add,
                                             op1=ALU.mult).then_inc(work_free[bank], 1)
                if name == "up":
                    gb, gt = WORK["gate", b]
                    dve.wait_ge(work_free[gb], gt + 1)
                    dve.wait_ge(work_ready[bank], turn + 1)
                    dve.tensor_tensor(gu[:], work[bank][:], gu[:], ALU.mult).then_inc(work_free[bank], 1)
                if name == "wsel":
                    ub, ut = WORK["up", b]
                    dve.wait_ge(work_free[ub], ut + 1)
                    dve.wait_ge(work_ready[bank], turn + 1)
                    if b:
                        db, dt = WORK["down", b - 1]
                        dve.wait_ge(work_ready[db], dt + 1)
                    dve.tensor_tensor(gated[:], work[bank][:], gu[:], ALU.mult).then_inc(work_free[bank], 1)
                if name == "wsel2":
                    lb_, lt = WORK["lora", b]
                    dve.wait_ge(work_free[lb_], lt + 1)
                    dve.wait_ge(work_ready[bank], turn + 1)
                    dve.tensor_tensor(lrw[:], work[bank][:, 0], lr[:], ALU.mult).then_inc(work_free[bank], 1)
                if name == "down":
                    dve.wait_ge(work_ready[bank], turn + 1)
                    if b >= 2:
                        dve.wait_ge(stored[b - 2], 16)
                    dve.tensor_tensor(res[:, b % 2], work[bank][:], x2[:, b % 2], ALU.add).then_inc(work_free[bank], 1)

        @block.tensor
        def _(pe):
            def product(dst, left, right, terms=((0, 0), (0, 1), (1, 0))):
                steps = [(k, i, j) for i, j in terms for k in range(KT)]
                for n, (k, i, j) in enumerate(steps):
                    ins = pe.matmul(dst, left(i, k), right(j, k), start=(n == 0), stop=(n == len(steps) - 1))
                return ins

            wap, wfp, cp = (wa_hi, wa_lo), (wf_hi, wf_lo), (cT_hi, cT_lo)
            xp = (xT_hi, xT_lo)
            for name, b, i in ORDER:
                if (name, b) in WORK:
                    bank, turn = WORK[name, b]
                    dst = work[bank]
                    if turn:
                        pe.wait_ge(work_free[bank], turn)
                if name in ("xT", "x2T"):
                    w = int(name == "x2T")
                    if LN[w, b] == 0:
                        pe.wait_ge(consts, 2)
                    pe.wait_ge(xn_ready, LN[w, b] + 1)
                    for k in range(KT):
                        for t in range(ST):
                            ins = pe.transpose(dst[:, k, t * P:(t + 1) * P], xn[:, w, t, k * P:(k + 1) * P], ident[:])
                    ins.then_inc(work_ready[bank], 1)
                if name == "k":
                    pe.wait_ge(wa_lo_ready, 1)
                    pe.wait_ge(c_ready, b + 1)
                    for o in range(KT):
                        ins = product(dst[:, o], lambda i, k: wap[i][:, k, o * P:(o + 1) * P], lambda j, k: cp[j][:, k])
                    ins.then_inc(work_ready[bank], 1)
                if name == "q":
                    pe.wait_ge(wa_lo_ready, 2)
                    xb, xt_ = WORK["xT", b]
                    pe.wait_ge(work_free[xb], xt_ + 1)
                    for o in range(KT):
                        ins = product(dst[:, o], lambda i, k: wap[i][:, k, D + o * P:D + (o + 1) * P],
                                      lambda j, k: xp[j][:, 0, k])
                    ins.then_inc(work_ready[bank], 1)
                if name == "v":
                    pe.wait_ge(wa_lo_ready, 3)
                    for t in range(TT):
                        ins = product(dst[:, t], lambda i, k: cp[i][:, k, t * P:(t + 1) * P],
                                      lambda j, k: wap[j][:, k, 2 * D:3 * D])
                    ins.then_inc(work_ready[bank], 1)
                if name == "max":
                    n = HEADS * b + i
                    if i == 0:
                        pe.wait_ge(k_stacked[b % NSTACK], 96 * (b // NSTACK + 1))
                        pe.wait_ge(q_stacked[b % NSTACK], 48 * (b // NSTACK + 1))
                    if n >= 2:
                        pe.wait_ge(max_done, n - 1)
                    ks, qs = kstack[b % NSTACK], qstack[b % NSTACK]
                    for t in range(ST):
                        ins = pe.matmul(s_bank[n % 2][:, t], qs[0:ROWS, i // 2, t * P:(t + 1) * P], ks[0:ROWS, i],
                                        start=True, stop=True)
                    ins.then_inc(s_ready, 1)
                if name == "mrow":
                    pe.wait_ge(max_done, HEADS * (b + 1))
                    for t in range(ST):
                        ins = pe.transpose(dst[0:HEADS, 0, t * P:(t + 1) * P], rowmax[:, b % 2, t], ident[:])
                    ins.then_inc(work_ready[bank], 1)
                if name == "attn":
                    n = HEADS * b + i
                    if n >= 2:
                        pe.wait_ge(exp_done, n - 1)
                    if i == 0:
                        mb, mt = WORK["mrow", b]
                        pe.wait_ge(work_free[mb], mt + 1)
                    elif i % 2 == 0:
                        pe.wait_ge(mrow_ready, (PAIRS - 1) * b + i // 2)
                    ks, qs = kstack[b % NSTACK], qstack[b % NSTACK]
                    for t in range(TT):
                        ins = pe.matmul(t_bank[n % 2][:, t], ks[0:MROW, i, t * P:(t + 1) * P], qs[0:MROW, i // 2],
                                        start=True, stop=True)
                    ins.then_inc(t_ready, 1)
                if name == "pv":
                    n = GROUPS * b + i
                    pe.wait_ge(exp_done, HEADS * b + 4 * i + 4)
                    if n:
                        pe.wait_ge(u_read, n)
                    if i == 0:
                        vb, vt = WORK["v", b]
                        pe.wait_ge(work_free[vb], vt + 1)
                        pe.wait_ge(vones, 3)
                    for t in range(TT):
                        for j in range(4):
                            h = 4 * i + j
                            ins = pe.matmul(u_bank[QUAD * j:QUAD * (j + 1), 0], vaug[:, b % 3, t, h],
                                            probs[:, (HEADS * b + h) % NPROB, t], start=(t == 0), stop=(t == TT - 1),
                                            tile_position=(0, QUAD * j))
                    ins.then_inc(pv_done, 1)
                if name == "o":
                    pe.wait_ge(wo_in, 16)
                    pe.wait_ge(attn_ready, 2 * (b + 1))
                    for t in range(ST):
                        for k in range(2):
                            ins = pe.matmul(dst[:, t], attnT[:, k, t * P:(t + 1) * P], wo[:, k], start=(k == 0),
                                            stop=(k == 1))
                    ins.then_inc(work_ready[bank], 1)
                if name in ("logits", "gate", "up", "lora"):
                    if name == "logits":
                        pe.wait_ge(wf_ready, 1)
                        xb, xt_ = WORK["x2T", b]
                        pe.wait_ge(work_free[xb], xt_ + 1)
                    first, width, tiles = {"gate": (0, P, 2), "up": (EF, P, 2), "lora": (2 * EF, P, 1),
                                           "logits": (2 * EF + ER, QUAD, 1)}[name]
                    for o in range(tiles):
                        at = first + o * P
                        ins = product(dst[0:width, o], lambda i, k: wfp[i][:, k, at:at + width],
                                      lambda j, k: xp[j][:, 1, k])
                    ins.then_inc(work_ready[bank], 1)
                if name in ("wsel", "wsel2"):
                    pe.wait_ge(wT_ready, b + 1)
                    for o, k in enumerate((0, 1) if name == "wsel" else (2,)):
                        for n, part in enumerate((wT_hi, wT_lo)):
                            ins = pe.matmul(dst[:, o], sel[:, k], part[:], start=(n == 0), stop=(n == 1))
                    ins.then_inc(work_ready[bank], 1)
                if name == "down":
                    if b == 0:
                        pe.wait_ge(wd_in, 32)
                    for st in ("wsel", "wsel2"):
                        sb_, s_t = WORK[st, b]
                        pe.wait_ge(work_free[sb_], s_t + 1)
                    for t in range(ST):
                        at = slice(t * P, (t + 1) * P)
                        pe.matmul(dst[:, t], gated[:, 0, at], wd[:, 0], start=True, stop=False)
                        pe.matmul(dst[:, t], gated[:, 1, at], wd[:, 1], start=False, stop=False)
                        ins = pe.matmul(dst[:, t], lrw[:, at], lb[:], start=False, stop=True)
                    ins.then_inc(work_ready[bank], 1)


def kernel(**inputs):
    import numpy as np
    import concourse.bacc as bacc
    from concourse.bass_utils import run_bass_kernel_spmd as run

    a = {k: np.asarray(v) for k, v in inputs.items()}
    flat = lambda w: w.reshape(-1, w.shape[-1]).T
    wo = a["L0_xattn_Wo"].T.reshape(2, 2, 4, HD, D).transpose(2, 1, 3, 0, 4)
    arrays = {
        "x": a["x"],
        "ctxT": a["ctx_2048"].transpose(0, 2, 1),
        "wattn": np.concatenate([a["L0_xattn_Wk"].T, a["L0_xattn_Wq"].T, a["L0_xattn_Wv"].T], 1),
        "wffn": np.concatenate([flat(a["L0_ffn_gate_w"]), flat(a["L0_ffn_up_w"]), flat(a["L0_ffn_lora_A"]),
                                a["L0_ffn_G"]], 1),
        "woT": wo.reshape(P, 2, D),
        "wdown": a["L0_ffn_down_w"].transpose(0, 2, 1).reshape(EF, D),
        "loraB": a["L0_ffn_lora_B"].transpose(0, 2, 1).reshape(ER, D),
        "bq": a["L0_xattn_bq"].reshape(KT, P).T, "bk": a["L0_xattn_bk"].reshape(KT, P).T,
         "bv": a["L0_xattn_bv"], "bo": a["L0_xattn_bo"],
    }
    nc = bacc.Bacc("TRN2", target_bir_lowering=False, num_devices=1)
    args = []
    for name, v in arrays.items():
        arrays[name] = v = np.ascontiguousarray(v)
        args.append(nc.dram_tensor(name, v.shape, mybir.dt.from_np(v.dtype), kind="ExternalInput").ap())
    args.append(nc.dram_tensor("out", [B, S, D], F32, kind="ExternalOutput").ap())
    xattn_moe_kernel(nc, *args)
    r = run(nc, [arrays], core_ids=[0])
    return r.results[0]["out"]
```

```python
from contextlib import ExitStack

import concourse.bass as bass
from concourse import mybir

F32 = mybir.dt.float32
F32R = mybir.dt.float32r
ALU = mybir.AluOpType
ACT = mybir.ActivationFunctionType
AX = mybir.AxisListType

P = 128
B, S, T, D = 4, 256, 256, 256
HEADS = 16
HD = D // HEADS
PAIRS = HEADS // 2
E, F, R = 8, 32, 16
EF, ER = E * F, E * R
KT = D // P
ST = S // P
TT = T // P
QUAD = 32
GROUPS = HEADS // 4
BLK = S // QUAD
EPS = 1e-5
SCALE = HD ** -0.5
NSTACK = 3
NPROB = 8
NWORK = 3
ROWS = 3 * QUAD
MROW = ROWS + HEADS

WORK_STAGES = {"xT", "k", "q", "v", "mrow", "o", "x2T", "low", "glu0", "glu1", "hT", "lT", "down"}
WARM = {"start": 16, "x2T": 12, "low": 6, "hT": 8, "down": 2}
ORDERS = {
    "tensor": """
        k:0 xT:0 k:1 q:0 v:0 xT:1 v:1 q:1 max:0.0-10 bias:0 max:0.11-15 max:1.0-1 mrow:0 attn:0.0-1
        max:1.2-5 attn:0.2-3 max:1.6 xT:2 attn:0.4-5 max:1.7-8 attn:0.6 q:2 k:2 attn:0.7 pv:0.0
        attn:0.8 max:1.9 attn:0.9 max:1.10 k:3 attn:0.10 pv:0.1 attn:0.11-12 max:1.11-12 xT:3
        attn:0.13-14 pv:0.2 attn:0.15 max:1.13-14 v:2 pv:0.3 max:1.15 q:3 max:2.0 mrow:1 max:2.1 o:0
        max:2.2-3 attn:1.0-1 max:2.4-5 attn:1.2 max:2.6 attn:1.3 max:2.7-8 pv:1.0 max:2.9-10
        attn:1.4-5 v:3 max:2.11 attn:1.6 max:2.12 attn:1.7 max:2.13 attn:1.8 max:2.14 attn:1.9
        max:2.15 attn:1.10 max:3.0 attn:1.11 mrow:2 max:3.1 attn:1.12-13 pv:1.1 max:3.2-3
        attn:1.14-15 pv:1.2 max:3.4-5 attn:2.0-1 pv:1.3 max:3.6-7 attn:2.2-3 x2T:0 max:3.8 attn:2.4
        max:3.9 attn:2.5 max:3.10 attn:2.6 max:3.11 attn:2.7-9 pv:2.0 max:3.12-13 o:1 max:3.14-15
        attn:2.10-11 pv:2.1 mrow:3 attn:2.12-13 low:0 attn:2.14-15 glu0:0 pv:2.2 attn:3.0-1 glu1:0
        attn:3.2 pv:2.3 attn:3.3-4 x2T:1 attn:3.5-7 pv:3.0 o:2 hT:0 pv:3.1 lT:0 attn:3.8-9 low:1
        attn:3.10-11 glu0:1 attn:3.12 pv:3.2 attn:3.13-14 glu1:1 attn:3.15 x2T:2 down:0 pv:3.3 hT:1
        lT:1 low:2 o:3 glu0:2 glu1:2 down:1 x2T:3 hT:2 lT:2 low:3 glu0:3 glu1:3 down:2 hT:3 lT:3
        down:3
    """,
    "vector": """
        ln1:0 ctx:0 wk:0 norm1:0 ctx:1 wq:0 ln1:1 xT:0 k:0 wv:0 q:0 norm1:1 k:1 xT:1 q:1 max:0.0-8
        ln1:2 max:0.9-15 ln1:3 max:1.0-4 norm1:2 max:1.5-6 xT:2 max:1.7-8 bias:0 norm1:3 q:2 k:2
        pv:0.0 max:1.9-10 pv:0.1 max:1.11-12 k:3 pv:0.2 max:1.13-14 xT:3 max:1.15 pv:0.3 max:2.0-1
        q:3 max:2.2-8 o:0 ln2:0 max:2.9-15 pv:1.0 max:3.0-1 pv:1.1 max:3.2-3 pv:1.2 max:3.4-5
        norm2:0 max:3.6-9 pv:1.3 max:3.10-11 x2T:0 max:3.12-13 pv:2.0 max:3.14-15 o:1 ln2:1 pv:2.1
        norm2:1 route1:0 route2:0 pv:2.2 route3:0 glu0:0 pv:2.3 glu1:0 weigh:0 pv:3.0 x2T:1 o:2
        ln2:2 pv:3.1 norm2:2 route1:1 route2:1 glu0:1 pv:3.2 route3:1 glu1:1 x2T:2 weigh:1 down:0
        pv:3.3 route1:2 route2:2 o:3 ln2:3 glu0:2 route3:2 glu1:2 norm2:3 weigh:2 down:1 x2T:3
        route1:3 route2:3 glu0:3 route3:3 glu1:3 weigh:3 down:2 down:3
    """,
    "scalar": """
        wk:0 wq:0 wv:0 k:0 xT:0 q:0 v:0 k:1 xT:1 v:1 q:1 mrow:0 attn:0.0-3 xT:2 attn:0.4-6 q:2 k:2
        attn:0.7-12 k:3 attn:0.13-15 xT:3 v:2 q:3 mrow:1 attn:1.0-5 v:3 attn:1.6-11 mrow:2
        attn:1.12-15 attn:2.0-7 x2T:0 attn:2.8-11 mrow:3 attn:2.12-13 low:0 attn:2.14-15 glu0:0
        exps:0 attn:3.0-1 glu1:0 attn:3.2-7 x2T:1 hT:0 lT:0 attn:3.8-9 low:1 attn:3.10-11 exps:1
        glu0:1 attn:3.12-14 glu1:1 attn:3.15 x2T:2 hT:1 lT:1 low:2 exps:2 glu0:2 glu1:2 x2T:3 hT:2
        lT:2 low:3 exps:3 glu0:3 glu1:3 hT:3 lT:3
    """,
    "gpsimd": """
        zeros:0 ones:0 ln1:0 zeros:1 minus:0 ln1:1 zeros:2 minus:1 minus:2 consts:0 ln1:2 ctx:2
        ln1:3 ctx:3 xo:0 xo:1 ln2:0 xo:2 ln2:1 xo:3 ln2:2 ln2:3
    """,
    "sync": """
        k:0 q:0 kload:0 qload:0 k:1 q:1 loads:0 qload:1 kload:1 ctx:2 ctx:3 mrow:0 q:2 k:2 qload:2
        kload:2 k:3 kload:3 mrow:1 q:3 qload:3 mrow:2 mrow:3 down:0 down:1 down:2 down:3
    """,
}


def plan(engine):
    stages = []
    for word in ORDERS[engine].split():
        name, _, at = word.partition(":")
        item, _, steps = at.partition(".")
        first, _, last = (steps or "0").partition("-")
        stages += [(name, int(item), i) for i in range(int(first), int(last or first) + 1)]
    return stages


def xattn_moe_kernel(nc, x, ctxT, wattn, wffn, woT, wdown, loraB, bq, bk, bv, bo, out):
    ORDER = plan("tensor")
    WORK, used = {}, 0
    for name, b, _ in ORDER:
        if name in WORK_STAGES:
            WORK[name, b] = (used % NWORK, used // NWORK)
            used += 1

    WEIGHTS = {name: (n, slice(n * D, (n + 1) * D)) for n, name in enumerate(("wk", "wq", "wv"))}

    with ExitStack() as ctx:
        def sb(name, shape, dt=F32):
            return ctx.enter_context(nc.sbuf_tensor(name, shape, dt))

        def sem(name):
            return ctx.enter_context(nc.semaphore(name))

        s_bank = [ctx.enter_context(nc.psum_tensor(f"s_bank{i}", [P, ST, T], F32)) for i in range(2)]
        t_bank = [ctx.enter_context(nc.psum_tensor(f"t_bank{i}", [P, TT, S], F32)) for i in range(2)]
        u_bank = ctx.enter_context(nc.psum_tensor("u_bank", [P, 2, S], F32))
        work = [ctx.enter_context(nc.psum_tensor(f"work{i}", [P, 2, S], F32)) for i in range(NWORK)]

        WA, WF = 3 * D, 2 * EF + ER + E
        wa_hi, wa_lo = sb("wa_hi", [P, KT, WA], F32R), sb("wa_lo", [P, KT, WA], F32R)
        wf_hi, wf_lo = sb("wf_hi", [P, KT, WF], F32R), sb("wf_lo", [P, KT, WF], F32R)
        wo = sb("wo", [P, KT, D])
        wd = sb("wd", [P, EF // P, D])
        lb = sb("lb", [P, D])
        bq_sb, bk_sb = sb("bq_sb", [P, KT]), sb("bk_sb", [P, KT])
        bv_sb, bo_sb = sb("bv_sb", [P, KT]), sb("bo_sb", [P, D])
        ident = sb("ident", [P, P])
        earlier = sb("earlier", [P, E, E])
        mhalf = sb("mhalf", [P, ST])

        xs = sb("xs", [P, B, ST, D])
        xo = sb("xo", [P, 2, ST, D])
        cT = sb("cT", [P, 2, KT, T])
        cT_hi, cT_lo = sb("cT_hi", [P, 2, KT, T], F32R), sb("cT_lo", [P, 2, KT, T], F32R)
        stats = sb("stats", [P, 2, B, ST, 6])
        mv = sb("mv", [P, 2, B, ST, 2])
        vare = sb("vare", [P, 2, B, ST])
        rstd = sb("rstd", [P, 2, B, ST])
        xn = sb("xn", [P, 2, ST, D])
        xT_hi, xT_lo = sb("xT_hi", [P, 2, KT, S], F32R), sb("xT_lo", [P, 2, KT, S], F32R)
        k_hi, k_lo = sb("k_hi", [P, KT, T], F32R), sb("k_lo", [P, KT, T], F32R)
        q_hi, q_lo = sb("q_hi", [P, KT, S], F32R), sb("q_lo", [P, KT, S], F32R)
        vaug = sb("vaug", [P, 3, TT, HEADS, QUAD])
        kstack = [sb(f"kstack{i}", [P, HEADS, T], F32R) for i in range(NSTACK)]
        qstack = [sb(f"qstack{i}", [P, PAIRS, S], F32R) for i in range(NSTACK)]
        rowmax = sb("rowmax", [P, 2, ST, HEADS])
        probs = sb("probs", [P, NPROB, TT, S])
        flat_probs = probs[:].rearrange("p n t s -> p (n t s)")
        wa = flat_probs[:, 0:KT * WA].rearrange("p (k o) -> p k o", k=KT)
        wf = flat_probs[:, KT * WA:KT * (WA + WF)].rearrange("p (k o) -> p k o", k=KT)
        uT = sb("uT", [P, GROUPS, BLK, QUAD])
        rden = sb("rden", [P, GROUPS, BLK])
        un = sb("un", [P, 2, BLK, 2, HD])
        attnT = sb("attnT", [P, 2, S])
        x2 = xs
        low = sb("low", [P, ST, ER + E])
        top = sb("top", [P, ST])
        below, ex, rank = sb("below", [P, ST, E]), sb("ex", [P, ST, E]), sb("rank", [P, ST, E])
        ahead, tied = sb("ahead", [P, ST, E, E]), sb("tied", [P, ST, E, E])
        esum, einv = sb("esum", [P, ST]), sb("einv", [P, ST])
        wexp = sb("wexp", [P, ST, E])
        th = sb("th", [P, ST, EF])
        hid = sb("hid", [P, ST, EF])
        hidT = sb("hidT", [P, EF // P, S])
        lw = sb("lw", [P, ST, ER])
        lT = sb("lT", [P, S])
        res = sb("res", [P, 2, ST, D])

        k_parts = nc.dram_tensor("k_parts", [2, 2, D, T], F32, kind="Internal").ap()
        q_parts = nc.dram_tensor("q_parts", [2, 2, D, S], F32, kind="Internal").ap()

        x_in = [sem(f"x_in{b}") for b in range(B)]
        c_in = [sem(f"c_in{b}") for b in range(B)]
        wk_in, wq_in, wv_in, wf_in = sem("wk_in"), sem("wq_in"), sem("wv_in"), sem("wf_in")
        bias_in, value_bias_in = sem("bias_in"), sem("value_bias_in")
        wo_in, wd_in = sem("wo_in"), sem("wd_in")
        consts, earlier_ready = sem("consts"), sem("earlier_ready")
        kzero, khalf, kminus = sem("kzero"), sem("khalf"), sem("kminus")
        vones = sem("vones")
        wa_hi_ready, wa_lo_ready = sem("wa_hi_ready"), sem("wa_lo_ready")
        wf_ready = sem("wf_ready")
        work_ready = [sem(f"work_ready{i}") for i in range(NWORK)]
        work_free = [sem(f"work_free{i}") for i in range(NWORK)]
        moments = [sem(f"moments{w}") for w in (1, 2)]
        rstd_ready = [sem(f"rstd_ready{w}") for w in (1, 2)]
        xn_ready = [sem(f"xn_ready{w}") for w in (1, 2)]
        dve_chain = sem("dve_chain")
        pool_chain = sem("pool_chain")
        hi_ready = [sem(f"hi_ready{w}") for w in (1, 2)]
        c_ready = sem("c_ready")
        khi_ready, qhi_ready = sem("khi_ready"), sem("qhi_ready")
        k_stored, q_stored = sem("k_stored"), sem("q_stored")
        k_stacked = [sem(f"k_stacked{i}") for i in range(NSTACK)]
        q_stacked = [sem(f"q_stacked{i}") for i in range(NSTACK)]
        s_ready, max_done = sem("s_ready"), sem("max_done")
        mrow_ready = [sem(f"mrow_ready{b}") for b in range(B)]
        t_ready, exp_done = sem("t_ready"), sem("exp_done")
        pv_done, u_read = sem("pv_done"), sem("u_read")
        attn_ready = sem("attn_ready")
        bias_product, bias_ready = sem("bias_product"), sem("bias_ready")
        xo_ready = sem("xo_ready")
        below_ready, e_ready = sem("below_ready"), sem("e_ready")
        th_ready = sem("th_ready")
        weighed = sem("weighed")
        stored = [sem(f"stored{b}") for b in range(B)]

        block = ctx.enter_context(nc.Block())

        @block.sync
        def _(sp):
            wview = wattn.rearrange("(k p) o -> p k o", p=P)
            sp.dma_start(xs[:, 0], x[0].rearrange("(t p) d -> p t d", p=P)).then_inc(x_in[0], 16)
            sp.dma_start(wa[:, :, 0:D], wview[:, :, 0:D]).then_inc(wk_in, 16)
            sp.dma_start(wa[:, :, D:2 * D], wview[:, :, D:2 * D]).then_inc(wq_in, 16)
            sp.dma_start(cT[:, 1], ctxT[1].rearrange("(k p) t -> p k t", p=P)).then_inc(c_in[1], 16)
            sp.dma_start(wa[:, :, 2 * D:3 * D], wview[:, :, 2 * D:3 * D]).then_inc(wv_in, 16)
            sp.dma_start(xs[:, 1], x[1].rearrange("(t p) d -> p t d", p=P)).then_inc(x_in[1], 16)
            sp.dma_start(bv_sb[:], bv).then_inc(value_bias_in, 16)
            sp.dma_start(bo_sb[:], bo.partition_broadcast(P)).then_inc(value_bias_in, 16)

            def later_loads():
                sp.dma_start(wo[:], woT).then_inc(wo_in, 16)
                sp.dma_start(wf, wffn.rearrange("(k p) o -> p k o", p=P)).then_inc(wf_in, 16)
                for b in range(2, B):
                    sp.dma_start(xs[:, b], x[b].rearrange("(t p) d -> p t d", p=P)).then_inc(x_in[b], 16)
                sp.dma_start(wd[:], wdown.rearrange("(k p) o -> p k o", p=P)).then_inc(wd_in, 16)
                sp.dma_start(lb[:], loraB).then_inc(wd_in, 16)

            for name, b, _ in plan("sync"):
                if name == "ctx" and b >= 2:
                    sp.wait_ge(c_ready, b - 1)
                    sp.dma_start(cT[:, b % 2], ctxT[b].rearrange("(k p) t -> p k t", p=P)).then_inc(c_in[b], 16)
                if name == "k":
                    if b >= 2:
                        sp.wait_ge(k_stacked[b - 2], 96)
                    sp.wait_ge(khi_ready, b + 1)
                    sp.dma_start(k_parts[b % 2, 0].rearrange("(k p) t -> p k t", p=P), k_hi[:].bitcast(F32)).then_inc(k_stored, 16)
                    bank, turn = WORK["k", b]
                    sp.wait_ge(work_free[bank], turn + 1)
                    sp.dma_start(k_parts[b % 2, 1].rearrange("(k p) t -> p k t", p=P), k_lo[:].bitcast(F32)).then_inc(k_stored, 16)
                if name == "kload":
                    sp.wait_ge(k_stored, 32 * (b + 1))
                    if b == 0:
                        sp.wait_ge(khalf, 1)
                    if b < NSTACK:
                        sp.wait_ge(kzero, b + 1)
                    else:
                        sp.wait_ge(t_ready, HEADS * (b - NSTACK + 1))
                    for g, part in enumerate((0, 0, 1)):
                        for half in range(2):
                            src = k_parts[b % 2, part].rearrange("(p h d) t -> h d p t", h=2, d=HD)[half]
                            lo = QUAD * g + HD * half
                            dst = kstack[b % NSTACK][lo:lo + HD].bitcast(F32).rearrange("d (p h) t -> d h p t", h=2)[:, half]
                            sp.dma_start(dst, src).then_inc(k_stacked[b % NSTACK], 16)
                if name == "q":
                    if b >= 2:
                        sp.wait_ge(q_stacked[b - 2], 48)
                    sp.wait_ge(qhi_ready, b + 1)
                    sp.dma_start(q_parts[b % 2, 0].rearrange("(k p) t -> p k t", p=P), q_hi[:].bitcast(F32)).then_inc(q_stored, 16)
                    bank, turn = WORK["q", b]
                    sp.wait_ge(work_free[bank], turn + 1)
                    sp.dma_start(q_parts[b % 2, 1].rearrange("(k p) t -> p k t", p=P), q_lo[:].bitcast(F32)).then_inc(q_stored, 16)
                if name == "qload":
                    sp.wait_ge(q_stored, 32 * (b + 1))
                    if b >= NSTACK:
                        sp.wait_ge(t_ready, HEADS * (b - NSTACK + 1))
                    for g, part in enumerate((0, 1, 0)):
                        sp.dma_start(qstack[b % NSTACK][QUAD * g:QUAD * (g + 1)].bitcast(F32),
                                     q_parts[b % 2, part].rearrange("(p r) s -> r p s", r=QUAD))\
                            .then_inc(q_stacked[b % NSTACK], 16)
                if name == "loads":
                    later_loads()
                if name == "mrow":
                    bank, turn = WORK["mrow", b]
                    sp.wait_ge(work_free[bank], turn + 1)
                    rows = qstack[b % NSTACK][ROWS:MROW].bitcast(F32)
                    sp.dma_start(rows[:, 2:PAIRS], rows[:, 0:1].to_broadcast([HEADS, PAIRS - 2, S]))\
                        .then_inc(mrow_ready[b], 16)
                if name == "down":
                    bank, turn = WORK["down", b]
                    sp.wait_ge(work_free[bank], turn + 1)
                    sp.dma_start(out[b].rearrange("(t p) d -> p t d", p=P), res[:, b % 2]).then_inc(stored[b], 16)
            for b in range(B):
                sp.wait_ge(stored[b], 16)

        @block.gpsimd
        def _(pool):
            chain = [0]

            def link(ins):
                chain[0] += 1
                ins.then_inc(pool_chain, 1)
                pool.wait_ge(pool_chain, chain[0])

            pool.memset(mhalf[:], -0.5).then_inc(consts, 1)
            link(pool.memset(ident[:], 0.0))
            pool.affine_select(out=ident[:], in_=ident[:], compare_op=ALU.not_equal, fill=1.0, base=0,
                               pattern=[[-1, P]], channel_multiplier=1).then_inc(consts, 1)
            pool.wait_ge(consts, 2)

            def context_parts(b):
                pool.wait_ge(c_in[b], 16)
                for reader in ("k", "v"):
                    bank, turn = WORK[reader, b - 2]
                    pool.wait_ge(work_ready[bank], turn + 1)
                link(pool.tensor_scalar(cT_hi[:, b % 2], cT[:, b % 2], 1.0, None, ALU.mult))
                pool.tensor_tensor(cT_lo[:, b % 2], cT[:, b % 2], cT_hi[:, b % 2].bitcast(F32), ALU.subtract)\
                    .then_inc(c_ready, 1)
                pool.wait_ge(c_ready, b + 1)

            def stack_constants(i):
                z = kstack[i][:].bitcast(F32)
                if i == 0:
                    z = z[:, HEADS // 2:]
                pool.memset(z, 0.0).then_inc(kzero, 1)
                pool.wait_ge(kzero, i + 1)

            def own_rows(i):
                if i == 0:
                    pool.wait_ge(khalf, 1)
                rows = kstack[i][ROWS:MROW]
                pool.affine_select(out=rows, in_=rows, compare_op=ALU.not_equal, fill=-1.0, base=0,
                                   pattern=[[-1, HEADS], [0, T]], channel_multiplier=1).then_inc(kminus, 1)
                pool.wait_ge(kminus, i + 1)

            def other_constants():
                link(pool.memset(earlier[:], 1.0))
                pool.affine_select(out=earlier[:], in_=earlier[:], compare_op=ALU.is_ge, fill=0.0, base=-1,
                                   pattern=[[1, E], [-1, E]], channel_multiplier=0).then_inc(earlier_ready, 1)
                pool.wait_ge(earlier_ready, 1)
                pool.wait_ge(wf_in, 16)
                link(pool.tensor_scalar(wf_hi[:], wf, 1.0, None, ALU.mult))
                pool.tensor_tensor(wf_lo[:], wf, wf_hi[:].bitcast(F32), ALU.subtract).then_inc(wf_ready, 1)
                pool.wait_ge(wf_ready, 1)

            for name, b, i in plan("gpsimd"):
                if name in ("ln1", "ln2"):
                    w = int(name == "ln2")
                    pool.wait_ge(moments[w], b + 1)
                    link(pool.tensor_scalar(vare[:, w, b], mv[:, w, b, :, 1], EPS, None, ALU.add))
                    pool.tensor_tensor(rstd[:, w, b], vare[:, w, b], mhalf[:], ALU.pow).then_inc(rstd_ready[w], 1)
                    pool.wait_ge(rstd_ready[w], b + 1)
                if name == "ctx" and b >= 2:
                    context_parts(b)
                if name == "minus":
                    own_rows(b)
                if name == "zeros":
                    stack_constants(b)
                if name == "ones":
                    for n in range(3):
                        pool.memset(vaug[:, n, :, :, HD:QUAD], 1.0).then_inc(vones, 1)
                    pool.wait_ge(vones, 3)
                if name == "consts":
                    other_constants()
                if name == "xo":
                    pool.wait_ge(bias_ready, 1)
                    if b >= 2:
                        pool.wait_ge(moments[1], b - 1)
                    for t in range(ST):
                        pool.tensor_tensor(xo[:, b % 2, t], xs[:, b, t], bo_sb[:], ALU.add).then_inc(xo_ready, 1)
                    pool.wait_ge(xo_ready, ST * (b + 1))

        @block.scalar
        def _(act):
            act.dma_start(cT[:, 0], ctxT[0].rearrange("(k p) t -> p k t", p=P)).then_inc(c_in[0], 16)
            act.dma_start(bk_sb[:], bk).then_inc(bias_in, 16)
            act.dma_start(bq_sb[:], bq).then_inc(bias_in, 16)
            for name, b, i in plan("scalar"):
                if (name, b) in WORK:
                    bank, turn = WORK[name, b]
                if name in WEIGHTS:
                    n, at = WEIGHTS[name]
                    act.wait_ge((wk_in, wq_in, wv_in)[n], 16)
                    act.copy(wa_hi[:, :, at], wa[:, :, at]).then_inc(wa_hi_ready, 1)
                if name in ("xT", "x2T"):
                    w = int(name == "x2T")
                    act.wait_ge(work_ready[bank], turn + 1)
                    act.copy(xT_hi[:, w], work[bank][:]).then_inc(hi_ready[w], 1)
                if name in ("k", "q"):
                    dst, bias, done, kept = (k_hi, bk_sb, khi_ready, k_stored) if name == "k" else (q_hi, bq_sb, qhi_ready, q_stored)
                    act.wait_ge(work_ready[bank], turn + 1)
                    act.wait_ge(bias_in, 32)
                    if b:
                        act.wait_ge(kept, 32 * b)
                    for o in range(KT):
                        ins = act.activation(dst[:, o], work[bank][:, o], ACT.Identity, bias=bias[:, o:o + 1])
                    ins.then_inc(done, 1)
                if name == "v":
                    act.wait_ge(work_ready[bank], turn + 1)
                    if b >= 3:
                        act.wait_ge(pv_done, GROUPS * (b - 2))
                    act.copy(vaug[:, b % 3, :, :, 0:HD], work[bank][:].rearrange("p t (h d) -> p t h d", d=HD))\
                        .then_inc(work_free[bank], 1)
                if name == "mrow":
                    act.wait_ge(work_ready[bank], turn + 1)
                    act.copy(qstack[b % NSTACK][ROWS:MROW, 0:2], work[bank][0:HEADS, 0:1].to_broadcast([HEADS, 2, S])).then_inc(work_free[bank], 1)
                if name == "attn":
                    n = HEADS * b + i
                    act.wait_ge(t_ready, n + 1)
                    if n == 0:
                        act.wait_ge(wa_lo_ready, 3)
                        act.wait_ge(wf_ready, 1)
                    if n >= NPROB:
                        act.wait_ge(pv_done, (n - NPROB) // 4 + 1)
                    act.activation(probs[:, n % NPROB], t_bank[n % 2][:], ACT.Exp, scale=SCALE).then_inc(exp_done, 1)
                if name == "low":
                    act.wait_ge(work_ready[bank], turn + 1)
                    if b:
                        act.wait_ge(weighed, 2 * b)
                    act.copy(low[:], work[bank][:, :, D - ER - E:D]).then_inc(work_free[bank], 1)
                if name == "exps":
                    act.wait_ge(below_ready, b + 1)
                    act.activation(ex[:], below[:], ACT.Exp).then_inc(e_ready, 1)
                if name in ("glu0", "glu1"):
                    act.wait_ge(work_ready[bank], turn + 1)
                    act.activation(th[:, int(name[3])], work[bank][:, 0], ACT.Tanh, scale=0.5).then_inc(th_ready, 1)
                if name in ("hT", "lT"):
                    act.wait_ge(work_ready[bank], turn + 1)
                    if b:
                        db, dt = WORK["down", b - 1]
                        act.wait_ge(work_ready[db], dt + 1)
                    if name == "hT":
                        act.copy(hidT[:], work[bank][:]).then_inc(work_free[bank], 1)
                    else:
                        act.copy(lT[:], work[bank][:, 0]).then_inc(work_free[bank], 1)

        @block.vector
        def _(dve):
            chain = [0]

            def link(ins):
                chain[0] += 1
                ins.then_inc(dve_chain, 1)
                dve.wait_ge(dve_chain, chain[0])

            dve.memset(kstack[0][:, 0:HEADS // 2].bitcast(F32), 0.0).then_inc(khalf, 1)

            def moments_of(src, w, b):
                for t in range(ST):
                    ins = dve.bn_stats(stats[:, w, b, t], src[:, t])
                link(ins)
                for t in range(ST):
                    ins = dve.bn_aggr(mv[:, w, b, t], stats[:, w, b, t])
                ins.then_inc(moments[w], 1)

            def wide(t):
                return t.unsqueeze(2).to_broadcast([P, ST, E])

            for name, b, i in plan("vector"):
                if (name, b) in WORK:
                    bank, turn = WORK[name, b]
                if name == "ctx" and b < 2:
                    dve.wait_ge(c_in[b], 16)
                    link(dve.tensor_copy(cT_hi[:, b], cT[:, b]))
                    dve.tensor_tensor(cT_lo[:, b], cT[:, b], cT_hi[:, b].bitcast(F32), ALU.subtract).then_inc(c_ready, 1)
                if name == "ln1":
                    dve.wait_ge(x_in[b], 16)
                    moments_of(xs[:, b], 0, b)
                if name in WEIGHTS:
                    n, at = WEIGHTS[name]
                    dve.wait_ge(wa_hi_ready, n + 1)
                    dve.tensor_tensor(wa_lo[:, :, at], wa[:, :, at], wa_hi[:, :, at].bitcast(F32),
                                      ALU.subtract).then_inc(wa_lo_ready, 1)
                if name in ("norm1", "norm2"):
                    w = int(name == "norm2")
                    src = x2[:, b] if w else xs[:, b]
                    dve.wait_ge(rstd_ready[w], b + 1)
                    if b:
                        tb, tt = WORK["x2T" if w else "xT", b - 1]
                        dve.wait_ge(work_ready[tb], tt + 1)
                    for t in range(ST):
                        ins = dve.tensor_scalar(xn[:, w, t], src[:, t], mv[:, w, b, t, 0:1], rstd[:, w, b, t:t + 1],
                                                ALU.subtract, ALU.mult)
                    ins.then_inc(xn_ready[w], 1)
                if name in ("xT", "x2T"):
                    w = int(name == "x2T")
                    dve.wait_ge(hi_ready[w], b + 1)
                    dve.tensor_tensor(xT_lo[:, w], work[bank][:], xT_hi[:, w].bitcast(F32), ALU.subtract)\
                        .then_inc(work_free[bank], 1)
                if name in ("k", "q"):
                    hi, lo, bias, up, kept = (k_hi, k_lo, bk_sb, khi_ready, k_stored) if name == "k" else \
                        (q_hi, q_lo, bq_sb, qhi_ready, q_stored)
                    if b:
                        dve.wait_ge(kept, 32 * b)
                    dve.wait_ge(up, b + 1)
                    for o in range(KT):
                        ins = dve.scalar_tensor_tensor(out=lo[:, o], in0=work[bank][:, o], scalar=bias[:, o:o + 1],
                                                       in1=hi[:, o].bitcast(F32), op0=ALU.add, op1=ALU.subtract)
                    ins.then_inc(work_free[bank], 1)
                if name == "bias":
                    dve.wait_ge(bias_product, 1)
                    dve.wait_ge(value_bias_in, 32)
                    dve.tensor_tensor(bo_sb[:], u_bank[:, 0], bo_sb[:], ALU.add).then_inc(bias_ready, 1)
                if name == "max":
                    n = HEADS * b + i
                    dve.wait_ge(s_ready, n + 1)
                    dve.tensor_reduce(rowmax[:, b % 2, :, i], s_bank[n % 2][:], AX.X, ALU.max).then_inc(max_done, 1)
                if name == "pv":
                    n = GROUPS * b + i
                    dve.wait_ge(pv_done, n + 1)
                    link(dve.transpose(uT[:, i], u_bank[:, 0]))
                    link(dve.reciprocal(rden[:, i], uT[:, i, :, HD]))
                    ins = dve.tensor_tensor(un[:, i // 2, :, i % 2], uT[:, i, :, 0:HD],
                                            rden[:, i].unsqueeze(2).to_broadcast([P, BLK, HD]), ALU.mult)
                    ins.then_inc(u_read, 1)
                    if i % 2:
                        dve.wait_ge(u_read, n + 1)
                        if b and i == 1:
                            ob, ot = WORK["o", b - 1]
                            dve.wait_ge(work_ready[ob], ot + 1)
                        dve.transpose(attnT[:, i // 2], un[:, i // 2]).then_inc(attn_ready, 1)
                if name == "o":
                    dve.wait_ge(work_ready[bank], turn + 1)
                    dve.wait_ge(xo_ready, ST * (b + 1))
                    ins = dve.tensor_tensor(x2[:, b], work[bank][:], xo[:, b % 2], ALU.add)
                    ins.then_inc(work_free[bank], 1)
                if name == "ln2":
                    ob, ot = WORK["o", b]
                    dve.wait_ge(work_free[ob], ot + 1)
                    moments_of(x2[:, b], 1, b)
                if name == "route1":
                    lb_, lt = WORK["low", b]
                    dve.wait_ge(work_free[lb_], lt + 1)
                    logit = low[:, :, ER:ER + E]
                    link(dve.tensor_reduce(top[:], logit, AX.X, ALU.max))
                    dve.tensor_tensor(below[:], logit, wide(top[:]), ALU.subtract).then_inc(below_ready, 1)
                    dve.wait_ge(below_ready, b + 1)
                if name == "route2":
                    if b == 0:
                        dve.wait_ge(earlier_ready, 1)
                    own = below[:].unsqueeze(3).to_broadcast([P, ST, E, E])
                    other = below[:].unsqueeze(2).to_broadcast([P, ST, E, E])
                    dve.tensor_tensor(tied[:], other, own, ALU.is_equal).then_inc(dve_chain, 1)
                    chain[0] += 1
                    dve.tensor_tensor(ahead[:], other, own, ALU.is_gt).then_inc(dve_chain, 1)
                    dve.wait_ge(dve_chain, chain[0])
                    chain[0] += 1
                    link(dve.tensor_tensor(tied[:], tied[:], earlier[:].unsqueeze(1).to_broadcast([P, ST, E, E]), ALU.mult))
                    link(dve.tensor_tensor(ahead[:], ahead[:], tied[:], ALU.add))
                if name == "route3":
                    link(dve.tensor_reduce(rank[:], ahead[:], AX.X, ALU.add))
                    dve.wait_ge(e_ready, b + 1)
                    link(dve.tensor_reduce(esum[:], ex[:], AX.X, ALU.add))
                    dve.reciprocal(einv[:], esum[:]).then_inc(dve_chain, 1)
                    chain[0] += 1
                    link(dve.scalar_tensor_tensor(out=ex[:], in0=rank[:], scalar=1.5, in1=ex[:], op0=ALU.is_lt,
                                                  op1=ALU.mult))
                    link(dve.tensor_tensor(wexp[:], ex[:], wide(einv[:]), ALU.mult))
                if name in ("glu0", "glu1"):
                    t = int(name[3])
                    dve.wait_ge(th_ready, ST * b + t + 1)
                    if b and t == 0:
                        tb, tt = WORK["hT", b - 1]
                        dve.wait_ge(work_ready[tb], tt + 1)
                    link(dve.scalar_tensor_tensor(out=hid[:, t], in0=th[:, t], scalar=1.0, in1=work[bank][:, 0],
                                                  op0=ALU.add, op1=ALU.mult))
                    dve.scalar_tensor_tensor(out=hid[:, t], in0=work[bank][:, 1], scalar=0.5, in1=hid[:, t],
                                             op0=ALU.mult, op1=ALU.mult).then_inc(work_free[bank], 1)
                if name == "weigh":
                    for st in ("glu0", "glu1"):
                        gb, gt = WORK[st, b]
                        dve.wait_ge(work_free[gb], gt + 1)
                    for t in range(ST):
                        ht = hid[:, t].rearrange("p (e f) -> p e f", e=E)
                        ins = dve.tensor_tensor(ht, ht, wexp[:, t].unsqueeze(2).to_broadcast([P, E, F]), ALU.mult)
                    ins.then_inc(weighed, 1)
                    if b:
                        tb, tt = WORK["lT", b - 1]
                        dve.wait_ge(work_ready[tb], tt + 1)
                    for t in range(ST):
                        lt_ = low[:, t, 0:ER].rearrange("p (e r) -> p e r", e=E)
                        ins = dve.tensor_tensor(lw[:, t].rearrange("p (e r) -> p e r", e=E), lt_,
                                                wexp[:, t].unsqueeze(2).to_broadcast([P, E, R]), ALU.mult)
                    ins.then_inc(weighed, 1)
                if name == "down":
                    dve.wait_ge(work_ready[bank], turn + 1)
                    if b >= 2:
                        dve.wait_ge(stored[b - 2], 16)
                    dve.tensor_tensor(res[:, b % 2], work[bank][:], x2[:, b], ALU.add).then_inc(work_free[bank], 1)

        @block.tensor
        def _(pe):
            def product(dst, left, right, terms=((0, 0), (0, 1), (1, 0))):
                steps = [(k, i, j) for i, j in terms for k in range(KT)]
                for n, (k, i, j) in enumerate(steps):
                    ins = pe.matmul(dst, left(i, k), right(j, k), start=(n == 0), stop=(n == len(steps) - 1))
                return ins

            def keep_warm(n):
                for _ in range(n):
                    pe.matmul(t_bank[0][:, 0, 0:P], ident[:], ident[:], start=True, stop=True)

            wap, wfp, cp = (wa_hi, wa_lo), (wf_hi, wf_lo), (cT_hi, cT_lo)
            xp = (xT_hi, xT_lo)
            pe.wait_ge(consts, 2)
            keep_warm(WARM["start"])
            for name, b, i in plan("tensor"):
                if (name, b) in WORK:
                    bank, turn = WORK[name, b]
                    dst = work[bank]
                    if turn:
                        pe.wait_ge(work_free[bank], turn)
                if b == B - 1 and name in WARM:
                    keep_warm(WARM[name])
                if name in ("xT", "x2T"):
                    w = int(name == "x2T")
                    pe.wait_ge(xn_ready[w], b + 1)
                    for k in range(KT):
                        for t in range(ST):
                            ins = pe.transpose(dst[:, k, t * P:(t + 1) * P], xn[:, w, t, k * P:(k + 1) * P], ident[:])
                    ins.then_inc(work_ready[bank], 1)
                if name == "k":
                    pe.wait_ge(wa_lo_ready, 1)
                    pe.wait_ge(c_ready, b + 1)
                    for o in range(KT):
                        ins = product(dst[:, o], lambda i, k: wap[i][:, k, o * P:(o + 1) * P], lambda j, k: cp[j][:, b % 2, k])
                    ins.then_inc(work_ready[bank], 1)
                if name == "q":
                    pe.wait_ge(wa_lo_ready, 2)
                    xb, xt_ = WORK["xT", b]
                    pe.wait_ge(work_free[xb], xt_ + 1)
                    for o in range(KT):
                        ins = product(dst[:, o], lambda i, k: wap[i][:, k, D + o * P:D + (o + 1) * P],
                                      lambda j, k: xp[j][:, 0, k])
                    ins.then_inc(work_ready[bank], 1)
                if name == "v":
                    pe.wait_ge(wa_lo_ready, 3)
                    pe.wait_ge(c_ready, b + 1)
                    for t in range(TT):
                        ins = product(dst[:, t], lambda i, k: cp[i][:, b % 2, k, t * P:(t + 1) * P],
                                      lambda j, k: wap[j][:, k, 2 * D:3 * D])
                    ins.then_inc(work_ready[bank], 1)
                if name == "bias":
                    pe.wait_ge(wo_in, 16)
                    pe.wait_ge(value_bias_in, 32)
                    for k in range(KT):
                        ins = pe.matmul(u_bank[:, 0], bv_sb[:, k:k + 1].to_broadcast([P, P]), wo[:, k],
                                        start=(k == 0), stop=(k == KT - 1))
                    ins.then_inc(bias_product, 1)
                if name == "max":
                    n = HEADS * b + i
                    if i == 0:
                        pe.wait_ge(k_stacked[b % NSTACK], 96 * (b // NSTACK + 1))
                        pe.wait_ge(q_stacked[b % NSTACK], 48 * (b // NSTACK + 1))
                    if n >= 2:
                        pe.wait_ge(max_done, n - 1)
                    ks, qs = kstack[b % NSTACK], qstack[b % NSTACK]
                    for t in range(ST):
                        ins = pe.matmul(s_bank[n % 2][:, t], qs[0:ROWS, i // 2, t * P:(t + 1) * P], ks[0:ROWS, i],
                                        start=True, stop=True)
                    ins.then_inc(s_ready, 1)
                if name == "mrow":
                    pe.wait_ge(max_done, HEADS * (b + 1))
                    for t in range(ST):
                        ins = pe.transpose(dst[0:HEADS, 0, t * P:(t + 1) * P], rowmax[:, b % 2, t], ident[:])
                    ins.then_inc(work_ready[bank], 1)
                if name == "attn":
                    n = HEADS * b + i
                    if n >= 2:
                        pe.wait_ge(exp_done, n - 1)
                    if i == 0:
                        mb, mt = WORK["mrow", b]
                        pe.wait_ge(work_free[mb], mt + 1)
                        if b < NSTACK:
                            pe.wait_ge(kminus, b + 1)
                    elif i == 4:
                        pe.wait_ge(mrow_ready[b], 16)
                    ks, qs = kstack[b % NSTACK], qstack[b % NSTACK]
                    for t in range(TT):
                        ins = pe.matmul(t_bank[n % 2][:, t], ks[0:MROW, i, t * P:(t + 1) * P], qs[0:MROW, i // 2],
                                        start=True, stop=True)
                    ins.then_inc(t_ready, 1)
                if name == "pv":
                    n = GROUPS * b + i
                    pe.wait_ge(exp_done, HEADS * b + 4 * i + 4)
                    if n:
                        pe.wait_ge(u_read, n)
                    if i == 0:
                        vb, vt = WORK["v", b]
                        pe.wait_ge(work_free[vb], vt + 1)
                        pe.wait_ge(vones, 3)
                        pe.wait_ge(bias_ready, 1)
                    for t in range(TT):
                        for j in range(4):
                            h = 4 * i + j
                            ins = pe.matmul(u_bank[QUAD * j:QUAD * (j + 1), 0], vaug[:, b % 3, t, h],
                                            probs[:, (HEADS * b + h) % NPROB, t], start=(t == 0), stop=(t == TT - 1),
                                            tile_position=(0, QUAD * j))
                    ins.then_inc(pv_done, 1)
                if name == "o":
                    pe.wait_ge(wo_in, 16)
                    pe.wait_ge(attn_ready, 2 * (b + 1))
                    for t in range(ST):
                        for k in range(2):
                            ins = pe.matmul(dst[:, t], attnT[:, k, t * P:(t + 1) * P], wo[:, k], start=(k == 0),
                                            stop=(k == 1))
                    ins.then_inc(work_ready[bank], 1)
                if name in ("low", "glu0", "glu1"):
                    if name == "low":
                        pe.wait_ge(wf_ready, 1)
                        xb, xt_ = WORK["x2T", b]
                        pe.wait_ge(work_free[xb], xt_ + 1)
                        for t in range(ST):
                            ins = product(dst[:, t], lambda i, k: xp[i][:, 1, k, t * P:(t + 1) * P],
                                          lambda j, k: wfp[j][:, k, WF - D:WF])
                    else:
                        t = int(name[3])
                        ins = product(dst[:].rearrange("p o f -> p (o f)"),
                                      lambda i, k: xp[i][:, 1, k, t * P:(t + 1) * P],
                                      lambda j, k: wfp[j][:, k, 0:2 * EF])
                    ins.then_inc(work_ready[bank], 1)
                if name == "hT":
                    pe.wait_ge(weighed, 2 * b + 1)
                    for k in range(EF // P):
                        for t in range(ST):
                            ins = pe.transpose(dst[:, k, t * P:(t + 1) * P], hid[:, t, k * P:(k + 1) * P], ident[:])
                    ins.then_inc(work_ready[bank], 1)
                if name == "lT":
                    pe.wait_ge(weighed, 2 * b + 2)
                    for t in range(ST):
                        ins = pe.transpose(dst[:, 0, t * P:(t + 1) * P], lw[:, t], ident[:])
                    ins.then_inc(work_ready[bank], 1)
                if name == "down":
                    if b == 0:
                        pe.wait_ge(wd_in, 32)
                    for st in ("hT", "lT"):
                        sb_, s_t = WORK[st, b]
                        pe.wait_ge(work_free[sb_], s_t + 1)
                    for t in range(ST):
                        at = slice(t * P, (t + 1) * P)
                        pe.matmul(dst[:, t], hidT[:, 0, at], wd[:, 0], start=True, stop=False)
                        pe.matmul(dst[:, t], hidT[:, 1, at], wd[:, 1], start=False, stop=False)
                        ins = pe.matmul(dst[:, t], lT[:, at], lb[:], start=False, stop=True)
                    ins.then_inc(work_ready[bank], 1)


def kernel(**inputs):
    import numpy as np
    import concourse.bacc as bacc
    from concourse.bass_utils import run_bass_kernel_spmd as run

    a = {k: np.asarray(v) for k, v in inputs.items()}
    flat = lambda w: w.reshape(-1, w.shape[-1]).T
    wo = a["L0_xattn_Wo"].T.reshape(2, 2, 4, HD, D).transpose(2, 1, 3, 0, 4)
    arrays = {
        "x": a["x"],
        "ctxT": a["ctx_2048"].transpose(0, 2, 1),
        "wattn": np.concatenate([a["L0_xattn_Wk"].T, a["L0_xattn_Wq"].T, a["L0_xattn_Wv"].T], 1),
        "wffn": np.concatenate([flat(a["L0_ffn_gate_w"]), flat(a["L0_ffn_up_w"]), flat(a["L0_ffn_lora_A"]),
                                a["L0_ffn_G"]], 1),
        "woT": wo.reshape(P, 2, D),
        "wdown": a["L0_ffn_down_w"].transpose(0, 2, 1).reshape(EF, D),
        "loraB": a["L0_ffn_lora_B"].transpose(0, 2, 1).reshape(ER, D),
        "bq": a["L0_xattn_bq"].reshape(KT, P).T, "bk": a["L0_xattn_bk"].reshape(KT, P).T,
        "bv": a["L0_xattn_bv"].reshape(2, 2, 4, HD).transpose(2, 1, 3, 0).reshape(P, 2), "bo": a["L0_xattn_bo"],
    }
    nc = bacc.Bacc("TRN2", target_bir_lowering=False, num_devices=1)
    args = []
    for name, v in arrays.items():
        arrays[name] = v = np.ascontiguousarray(v)
        args.append(nc.dram_tensor(name, v.shape, mybir.dt.from_np(v.dtype), kind="ExternalInput").ap())
    args.append(nc.dram_tensor("out", [B, S, D], F32, kind="ExternalOutput").ap())
    xattn_moe_kernel(nc, *args)
    r = run(nc, [arrays], core_ids=[0])
    return r.results[0]["out"]
```

```python
from contextlib import ExitStack

import concourse.bass as bass
from concourse import mybir

F32 = mybir.dt.float32
F32R = mybir.dt.float32r
ALU = mybir.AluOpType
ACT = mybir.ActivationFunctionType
AX = mybir.AxisListType

P = 128
B, S, T, D = 4, 256, 256, 256
HEADS = 16
HD = D // HEADS
PAIRS = HEADS // 2
E, F, R = 8, 32, 16
EF, ER = E * F, E * R
KT = D // P
ST = S // P
TT = T // P
QUAD = 32
GROUPS = HEADS // 4
BLK = S // QUAD
EPS = 1e-5
SCALE = HD ** -0.5
NSTACK = 3
NWARM = 6
NPROB = 8
NWORK = 3
ROWS = 3 * QUAD
MROW = ROWS + HEADS

WORK_STAGES = {"xT", "k", "q", "v", "mrow", "o", "x2T", "low", "glu0", "glu1", "hT", "lT", "down"}
ON_POOL = {("xT", 2), ("xT", 3), ("k", 2), ("k", 3), ("q", 2), ("q", 3), ("x2T", 0), ("x2T", 1), ("x2T", 2),
           ("weigh", 0), ("weigh", 1), ("weigh", 2)}
ORDERS = {
    "tensor": """
        xT:0 k:0 q:0 k:1 xT:1 q:1 v:0 v:1 max:0.0-5 xT:2 max:0.6-10 bias:0 max:0.11-12 q:2
        max:0.13-14 k:2 max:0.15 max:1.0 xT:3 max:1.1 mrow:0 max:1.2-3 attn:0.0-1 max:1.4 attn:0.2
        max:1.5 attn:0.3 max:1.6 k:3 max:1.7-8 attn:0.4 pv:0.0 attn:0.5-6 max:1.9-10 q:3 max:1.11
        attn:0.7 max:1.12 attn:0.8-9 max:1.13-14 pv:0.1 max:1.15 attn:0.10-11 max:2.0 mrow:1 max:2.1
        attn:0.12-13 max:2.2 v:2 max:2.3 attn:0.14 max:2.4 attn:0.15 pv:0.2 attn:1.0-1 max:2.5-6
        pv:0.3 max:2.7 attn:1.2 max:2.8 attn:1.3-4 max:2.9-10 attn:1.5 pv:1.0 attn:1.6-7 max:2.11-12
        attn:1.8-9 max:2.13 o:0 attn:1.10 max:2.14-15 attn:1.11 pv:1.1 attn:1.12-13 v:3 max:3.0-1
        mrow:2 pv:1.2 attn:1.14 max:3.2-3 attn:1.15 x2T:0 max:3.4 attn:2.0 max:3.5 attn:2.1-2
        max:3.6-7 attn:2.3 pv:1.3 max:3.8 attn:2.4 max:3.9 attn:2.5 low:0 max:3.10 attn:2.6 max:3.11
        attn:2.7 o:1 max:3.12 attn:2.8 max:3.13 pv:2.0 max:3.14 attn:2.9 max:3.15 glu0:0 attn:2.10
        mrow:3 attn:2.11 pv:2.1 attn:2.12-13 glu1:0 attn:2.14-15 pv:2.2 attn:3.0-1 x2T:1 attn:3.2-3
        pv:2.3 attn:3.4-5 pv:3.0 attn:3.6-7 o:2 attn:3.8-9 pv:3.1 attn:3.10 lT:0 low:1 attn:3.11-12
        glu0:1 attn:3.13-14 pv:3.2 hT:0 attn:3.15 glu1:1 x2T:2 pv:3.3 down:0 o:3 lT:1 low:2 hT:1
        glu0:2 glu1:2 down:1 x2T:3 hT:2 lT:2 low:3 glu0:3 glu1:3 down:2 hT:3 lT:3 down:3
    """,
    "vector": """
        ln1:0 ctx:0 norm1:0 wk:0 ctx:1 xT:0 wq:0 ln1:1 k:0 norm1:1 q:0 xT:1 ln1:2 ln1:3 wv:0 norm1:2
        k:1 ctx:2 q:1 max:0.0-12 norm1:3 max:0.13-14 bias:0 max:0.15 max:1.0-8 pv:0.0 max:1.9-15
        max:2.0-2 pv:0.1 max:2.3-4 pv:0.2 max:2.5-8 pv:0.3 max:2.9-13 pv:1.0 o:0 max:2.14 ln2:0
        max:2.15 pv:1.1 max:3.0-1 norm2:0 max:3.2-5 pv:1.2 max:3.6-9 pv:1.3 route1:0 max:3.10-11
        route2:0 max:3.12-15 pv:2.0 o:1 ln2:1 pv:2.1 glu0:0 norm2:1 pv:2.2 route3:0 glu1:0 pv:2.3
        pv:3.0 o:2 ln2:2 pv:3.1 route1:1 norm2:2 route2:1 glu0:1 pv:3.2 route3:1 glu1:1 pv:3.3
        down:0 o:3 ln2:3 route1:2 route2:2 norm2:3 route3:2 glu0:2 glu1:2 down:1 x2T:3 route1:3
        route2:3 glu0:3 route3:3 glu1:3 weigh:3 down:2 down:3
    """,
    "scalar": """
        wk:0 wq:0 xT:0 k:0 wv:0 q:0 xT:1 wf:0 k:1 qload:0 q:1 qload:0.1 v:0 v:1 xT:2 q:2 k:2 mrow:0
        attn:0.0-3 xT:3 attn:0.4-6 k:3 attn:0.7-9 q:3 attn:0.10-13 mrow:1 attn:0.14-15 attn:1.0 v:2
        attn:1.1-13 mrow:2 attn:1.14-15 v:3 attn:2.0-1 x2T:0 attn:2.2-5 low:0 attn:2.6-10 exps:0
        attn:2.11-13 glu0:0 mrow:3 attn:2.14-15 attn:3.0-1 glu1:0 attn:3.2-7 x2T:1 attn:3.8-10 low:1
        attn:3.11 exps:1 attn:3.12 lT:0 attn:3.13 glu0:1 attn:3.14-15 glu1:1 hT:0 x2T:2 lT:1 low:2
        exps:2 hT:1 glu0:2 glu1:2 x2T:3 hT:2 low:3 lT:2 glu0:3 exps:3 glu1:3 hT:3 lT:3
    """,
    "gpsimd": """
        ln1:0 zeros:0 ln1:1 minus:0 ln1:2 zeros:1 ln1:3 ctx:3 zeros:2 xT:2 consts:0 q:2 k:2 ones:0
        xT:3 q:3 xo:0 k:3 xo:1 ln2:0 x2T:0 ln2:1 xo:2 xo:3 weigh:0 x2T:1 ln2:2 weigh:1 x2T:2 ln2:3
        weigh:2
    """,
    "sync": """
        wf:0 xload:2 ctx:2 ctx:3 xload:3 k:0 q:0 kload:0 q:1 loads:0 k:1 minus:1 qload:1 kload:1 q:2
        mrow:0 minus:2 k:2 qload:2 kload:2 mrow:1 k:3 q:3 kload:3 qload:3 mrow:2 mrow:3 down:0
        down:1 down:2 down:3
    """,
}


def plan(engine):
    stages = []
    for word in ORDERS[engine].split():
        name, _, at = word.partition(":")
        item, _, steps = at.partition(".")
        first, _, last = (steps or "0").partition("-")
        stages += [(name, int(item), i) for i in range(int(first), int(last or first) + 1)]
    return stages


def xattn_moe_kernel(nc, x, ctxT, wattn, wffn, woT, wdown, loraB, bq, bk, bv, bo, out):
    WORK, used = {}, 0
    for name, b, _ in plan("tensor"):
        if name in WORK_STAGES:
            WORK[name, b] = (used % NWORK, used // NWORK)
            used += 1

    WEIGHTS = {name: (n, slice(n * D, (n + 1) * D)) for n, name in enumerate(("wk", "wq", "wv"))}

    with ExitStack() as ctx:
        def sb(name, shape, dt=F32):
            return ctx.enter_context(nc.sbuf_tensor(name, shape, dt))

        def sem(name):
            return ctx.enter_context(nc.semaphore(name))

        s_bank = [ctx.enter_context(nc.psum_tensor(f"s_bank{i}", [P, ST, T], F32)) for i in range(2)]
        t_bank = [ctx.enter_context(nc.psum_tensor(f"t_bank{i}", [P, TT, S], F32)) for i in range(2)]
        u_bank = ctx.enter_context(nc.psum_tensor("u_bank", [P, 2, S], F32))
        work = [ctx.enter_context(nc.psum_tensor(f"work{i}", [P, 2, S], F32)) for i in range(NWORK)]

        WA, WF = 3 * D, 2 * EF + ER + E
        wa_hi, wa_lo = sb("wa_hi", [P, KT, WA], F32R), sb("wa_lo", [P, KT, WA], F32R)
        wf_hi, wf_lo = sb("wf_hi", [P, KT, WF], F32R), sb("wf_lo", [P, KT, WF], F32R)
        wo = sb("wo", [P, KT, D])
        wd = sb("wd", [P, EF // P, D])
        lb = sb("lb", [P, D])
        bq_sb, bk_sb = sb("bq_sb", [P, KT]), sb("bk_sb", [P, KT])
        bv_sb, bo_sb = sb("bv_sb", [P, KT]), sb("bo_sb", [P, D])
        ident = sb("ident", [P, P])
        earlier = sb("earlier", [P, E, E])
        mhalf = sb("mhalf", [P, ST])

        xs = sb("xs", [P, B, ST, D])
        xo = sb("xo", [P, 2, ST, D])
        cT = sb("cT", [P, 2, KT, T])
        cT_hi, cT_lo = sb("cT_hi", [P, 2, KT, T], F32R), sb("cT_lo", [P, 2, KT, T], F32R)
        stats = sb("stats", [P, 2, B, ST, 6])
        mv = sb("mv", [P, 2, B, ST, 2])
        vare = sb("vare", [P, 2, B, ST])
        rstd = sb("rstd", [P, 2, B, ST])
        xn = sb("xn", [P, 2, ST, D])
        xT_hi, xT_lo = sb("xT_hi", [P, 2, KT, S], F32R), sb("xT_lo", [P, 2, KT, S], F32R)
        k_hi, k_lo = sb("k_hi", [P, KT, T], F32R), sb("k_lo", [P, KT, T], F32R)
        q_hi, q_lo = sb("q_hi", [P, KT, S], F32R), sb("q_lo", [P, KT, S], F32R)
        vaug = sb("vaug", [P, 3, TT, HEADS, QUAD])
        kstack = [sb(f"kstack{i}", [P, HEADS, T], F32R) for i in range(NSTACK)]
        qstack = [sb(f"qstack{i}", [P, PAIRS, S], F32R) for i in range(NSTACK)]
        rowmax = sb("rowmax", [P, 2, ST, HEADS])
        probs = sb("probs", [P, NPROB, TT, S])
        flat_probs = probs[:].rearrange("p n t s -> p (n t s)")
        wa = flat_probs[:, 0:KT * WA].rearrange("p (k o) -> p k o", k=KT)
        wf = flat_probs[:, KT * WA:KT * (WA + WF)].rearrange("p (k o) -> p k o", k=KT)
        uT = sb("uT", [P, GROUPS, BLK, QUAD])
        rden = sb("rden", [P, GROUPS, BLK])
        un = sb("un", [P, 2, BLK, 2, HD])
        attnT = sb("attnT", [P, 2, S])
        x2 = xs
        whole = {name: sb(f"{name}_whole", [P, 2, S]) for name in ("xT", "x2T", "k", "q")}
        low = sb("low", [P, ST, ER + E])
        top = sb("top", [P, ST])
        below, ex, rank = sb("below", [P, ST, E]), sb("ex", [P, ST, E]), sb("rank", [P, ST, E])
        ahead, tied = sb("ahead", [P, ST, E, E]), sb("tied", [P, ST, E, E])
        esum, einv = sb("esum", [P, ST]), sb("einv", [P, ST])
        wexp = sb("wexp", [P, ST, E])
        th = sb("th", [P, ST, EF])
        hid = sb("hid", [P, ST, EF])
        hidT = sb("hidT", [P, EF // P, S])
        lw = sb("lw", [P, ST, ER])
        lT = sb("lT", [P, S])
        res = sb("res", [P, 2, ST, D])

        k_parts = nc.dram_tensor("k_parts", [2, 2, D, T], F32, kind="Internal").ap()
        q_parts = nc.dram_tensor("q_parts", [2, 2, D, S], F32, kind="Internal").ap()

        x_in = [sem(f"x_in{b}") for b in range(B)]
        c_in = [sem(f"c_in{b}") for b in range(B)]
        wk_in, wq_in, wv_in, wf_in = sem("wk_in"), sem("wq_in"), sem("wv_in"), sem("wf_in")
        bias_in, value_bias_in = sem("bias_in"), sem("value_bias_in")
        wo_in, wd_in = sem("wo_in"), sem("wd_in")
        consts, earlier_ready = sem("consts"), sem("earlier_ready")
        kzero, khalf = sem("kzero"), sem("khalf")
        kminus = [sem(f"kminus{i}") for i in range(NSTACK)]
        vones = sem("vones")
        wa_hi_ready, wa_lo_ready = sem("wa_hi_ready"), sem("wa_lo_ready")
        wf_hi_ready, wf_ready = sem("wf_hi_ready"), sem("wf_ready")
        work_ready = [sem(f"work_ready{i}") for i in range(NWORK)]
        work_free = [sem(f"work_free{i}") for i in range(NWORK)]
        moments = [sem(f"moments{w}") for w in (1, 2)]
        rstd_ready = [sem(f"rstd_ready{w}") for w in (1, 2)]
        xn_ready = [sem(f"xn_ready{w}") for w in (1, 2)]
        dve_chain = sem("dve_chain")
        pool_chain = sem("pool_chain")
        hi_ready = [sem(f"hi_ready{w}") for w in (1, 2)]
        c_ready = sem("c_ready")
        khi_ready, qhi_ready = sem("khi_ready"), sem("qhi_ready")
        k_stored, q_stored = sem("k_stored"), sem("q_stored")
        k_stacked = [sem(f"k_stacked{i}") for i in range(NSTACK)]
        q_stacked = [sem(f"q_stacked{i}") for i in range(NSTACK)]
        pool_parts = {name: sem(f"{name}_parts") for name in ("xT", "x2T", "k", "q")}
        q_late = sem("q_late")
        s_ready, max_done = sem("s_ready"), sem("max_done")
        mrow_ready = [sem(f"mrow_ready{b}") for b in range(B)]
        t_ready, exp_done = sem("t_ready"), sem("exp_done")
        pv_done, u_read = sem("pv_done"), sem("u_read")
        attn_ready = sem("attn_ready")
        bias_product, bias_ready = sem("bias_product"), sem("bias_ready")
        xo_ready = sem("xo_ready")
        below_ready, e_ready = sem("below_ready"), sem("e_ready")
        th_ready = sem("th_ready")
        weights_ready, weighed = sem("weights_ready"), sem("weighed")
        stored = [sem(f"stored{b}") for b in range(B)]

        def pooled(name, b):
            return sum((name, n) in ON_POOL for n in range(b + 1))

        def wait_parts(engine, name, b):
            if (name, b) in ON_POOL:
                engine.wait_ge(pool_parts[name], pooled(name, b))
            else:
                bank, turn = WORK[name, b]
                engine.wait_ge(work_free[bank], turn + 1)

        def weigh(engine, b):
            engine.wait_ge(weights_ready, b + 1)
            for st in ("glu0", "glu1"):
                gb, gt = WORK[st, b]
                engine.wait_ge(work_free[gb], gt + 1)
            for t in range(ST):
                units = hid[:, t].rearrange("p (e f) -> p e f", e=E)
                ins = engine.tensor_tensor(units, units, wexp[:, t].unsqueeze(2).to_broadcast([P, E, F]), ALU.mult)
            ins.then_inc(weighed, 1)
            if b:
                tb, tt = WORK["lT", b - 1]
                engine.wait_ge(work_ready[tb], tt + 1)
            for t in range(ST):
                ins = engine.tensor_tensor(lw[:, t].rearrange("p (e r) -> p e r", e=E),
                                           low[:, t, 0:ER].rearrange("p (e r) -> p e r", e=E),
                                           wexp[:, t].unsqueeze(2).to_broadcast([P, E, R]), ALU.mult)
            ins.then_inc(weighed, 1)

        def wait_context(engine, b):
            engine.wait_ge(c_in[b], 16)
            if b >= 2:
                for reader in ("k", "v"):
                    bank, turn = WORK[reader, b - 2]
                    engine.wait_ge(work_ready[bank], turn + 1)

        def query_stack(engine, b, half):
            engine.wait_ge(q_stored, 32 * (b + 1))
            if b >= NSTACK:
                engine.wait_ge(t_ready, HEADS * (b - NSTACK + 1))
            pairs = slice(0, PAIRS) if b else (slice(0, PAIRS // 2), slice(PAIRS // 2, PAIRS))[half]
            for g, part in enumerate((0, 1, 0)):
                engine.dma_start(qstack[b % NSTACK][QUAD * g:QUAD * (g + 1), pairs].bitcast(F32),
                                 q_parts[b % 2, part].rearrange("(p r) s -> r p s", r=QUAD)[:, pairs])\
                    .then_inc(q_late if half else q_stacked[b % NSTACK], 16)

        block = ctx.enter_context(nc.Block())

        @block.sync
        def _(sp):
            wview = wattn.rearrange("(k p) o -> p k o", p=P)
            sp.dma_start(xs[:, 0], x[0].rearrange("(t p) d -> p t d", p=P)).then_inc(x_in[0], 16)
            sp.dma_start(wa[:, :, 0:D], wview[:, :, 0:D]).then_inc(wk_in, 16)
            sp.dma_start(wa[:, :, D:2 * D], wview[:, :, D:2 * D]).then_inc(wq_in, 16)
            sp.dma_start(cT[:, 1], ctxT[1].rearrange("(k p) t -> p k t", p=P)).then_inc(c_in[1], 16)
            sp.dma_start(wa[:, :, 2 * D:3 * D], wview[:, :, 2 * D:3 * D]).then_inc(wv_in, 16)
            sp.dma_start(xs[:, 1], x[1].rearrange("(t p) d -> p t d", p=P)).then_inc(x_in[1], 16)
            sp.dma_start(bv_sb[:], bv).then_inc(value_bias_in, 16)
            sp.dma_start(bo_sb[:], bo.partition_broadcast(P)).then_inc(value_bias_in, 16)

            def output_loads():
                sp.dma_start(wo[:], woT).then_inc(wo_in, 16)
                sp.dma_start(wd[:], wdown.rearrange("(k p) o -> p k o", p=P)).then_inc(wd_in, 16)
                sp.dma_start(lb[:], loraB).then_inc(wd_in, 16)

            for name, b, i in plan("sync"):
                if name == "ctx" and b >= 2:
                    sp.wait_ge(c_ready, b - 1)
                    sp.dma_start(cT[:, b % 2], ctxT[b].rearrange("(k p) t -> p k t", p=P)).then_inc(c_in[b], 16)
                if name == "k":
                    if b >= 2:
                        sp.wait_ge(k_stacked[b - 2], 96)
                    sp.wait_ge(khi_ready, b + 1)
                    sp.dma_start(k_parts[b % 2, 0].rearrange("(k p) t -> p k t", p=P), k_hi[:].bitcast(F32)).then_inc(k_stored, 16)
                    wait_parts(sp, "k", b)
                    sp.dma_start(k_parts[b % 2, 1].rearrange("(k p) t -> p k t", p=P), k_lo[:].bitcast(F32)).then_inc(k_stored, 16)
                if name == "kload":
                    sp.wait_ge(k_stored, 32 * (b + 1))
                    if b == 0:
                        sp.wait_ge(khalf, 1)
                    if b < NSTACK:
                        sp.wait_ge(kzero, b + 1)
                    else:
                        sp.wait_ge(t_ready, HEADS * (b - NSTACK + 1))
                    for g, part in enumerate((0, 0, 1)):
                        for half in range(2):
                            src = k_parts[b % 2, part].rearrange("(p h d) t -> h d p t", h=2, d=HD)[half]
                            lo = QUAD * g + HD * half
                            dst = kstack[b % NSTACK][lo:lo + HD].bitcast(F32).rearrange("d (p h) t -> d h p t", h=2)[:, half]
                            sp.dma_start(dst, src).then_inc(k_stacked[b % NSTACK], 16)
                if name == "q":
                    if b >= 2:
                        sp.wait_ge(q_stacked[b - 2], 48)
                        sp.wait_ge(q_late, 48)
                    sp.wait_ge(qhi_ready, b + 1)
                    sp.dma_start(q_parts[b % 2, 0].rearrange("(k p) t -> p k t", p=P), q_hi[:].bitcast(F32)).then_inc(q_stored, 16)
                    wait_parts(sp, "q", b)
                    sp.dma_start(q_parts[b % 2, 1].rearrange("(k p) t -> p k t", p=P), q_lo[:].bitcast(F32)).then_inc(q_stored, 16)
                if name == "qload":
                    query_stack(sp, b, i)
                if name == "xload":
                    sp.dma_start(xs[:, b], x[b].rearrange("(t p) d -> p t d", p=P)).then_inc(x_in[b], 16)
                if name == "wf":
                    sp.dma_start(wf, wffn.rearrange("(k p) o -> p k o", p=P)).then_inc(wf_in, 16)
                if name == "loads":
                    output_loads()
                if name == "minus":
                    sp.wait_ge(kminus[0], 1)
                    sp.wait_ge(kzero, b + 1)
                    sp.dma_start(kstack[b][ROWS:MROW].bitcast(F32), kstack[0][ROWS:MROW].bitcast(F32)).then_inc(kminus[b], 16)
                if name == "mrow":
                    bank, turn = WORK["mrow", b]
                    sp.wait_ge(work_free[bank], turn + 1)
                    rows = qstack[b % NSTACK][ROWS:MROW].bitcast(F32)
                    sp.dma_start(rows[:, 2:PAIRS], rows[:, 0:1].to_broadcast([HEADS, PAIRS - 2, S]))\
                        .then_inc(mrow_ready[b], 16)
                if name == "down":
                    bank, turn = WORK["down", b]
                    sp.wait_ge(work_free[bank], turn + 1)
                    sp.dma_start(out[b].rearrange("(t p) d -> p t d", p=P), res[:, b % 2]).then_inc(stored[b], 16)
            for b in range(B):
                sp.wait_ge(stored[b], 16)

        @block.gpsimd
        def _(pool):
            chain = [0]

            def link(ins):
                chain[0] += 1
                ins.then_inc(pool_chain, 1)
                pool.wait_ge(pool_chain, chain[0])

            pool.memset(mhalf[:], -0.5).then_inc(consts, 1)
            link(pool.memset(ident[:], 0.0))
            pool.affine_select(out=ident[:], in_=ident[:], compare_op=ALU.not_equal, fill=1.0, base=0,
                               pattern=[[-1, P]], channel_multiplier=1).then_inc(consts, 1)
            pool.wait_ge(consts, 2)

            def zero_stack(i):
                z = kstack[i][:].bitcast(F32)
                if i == 0:
                    z = z[:, HEADS // 2:]
                pool.memset(z, 0.0).then_inc(kzero, 1)
                pool.wait_ge(kzero, i + 1)

            def own_rows():
                pool.wait_ge(khalf, 1)
                rows = kstack[0][ROWS:MROW]
                pool.affine_select(out=rows, in_=rows, compare_op=ALU.not_equal, fill=-1.0, base=0,
                                   pattern=[[-1, HEADS], [0, T]], channel_multiplier=1).then_inc(kminus[0], 1)
                pool.wait_ge(kminus[0], 1)

            def other_constants():
                link(pool.memset(earlier[:], 1.0))
                pool.affine_select(out=earlier[:], in_=earlier[:], compare_op=ALU.is_ge, fill=0.0, base=-1,
                                   pattern=[[1, E], [-1, E]], channel_multiplier=0).then_inc(earlier_ready, 1)
                pool.wait_ge(earlier_ready, 1)
                pool.wait_ge(wf_hi_ready, 1)
                pool.tensor_tensor(wf_lo[:], wf, wf_hi[:].bitcast(F32), ALU.subtract).then_inc(wf_ready, 1)
                pool.wait_ge(wf_ready, 1)

            for name, b, i in plan("gpsimd"):
                if name in ("ln1", "ln2"):
                    w = int(name == "ln2")
                    pool.wait_ge(moments[w], b + 1)
                    link(pool.tensor_scalar(vare[:, w, b], mv[:, w, b, :, 1], EPS, None, ALU.add))
                    pool.tensor_tensor(rstd[:, w, b], vare[:, w, b], mhalf[:], ALU.pow).then_inc(rstd_ready[w], 1)
                    pool.wait_ge(rstd_ready[w], b + 1)
                if name in ("xT", "x2T", "k", "q"):
                    hi, lo = {"xT": (xT_hi[:, 0], xT_lo[:, 0]), "x2T": (xT_hi[:, 1], xT_lo[:, 1]),
                              "k": (k_hi[:], k_lo[:]), "q": (q_hi[:], q_lo[:])}[name]
                    bank, turn = WORK[name, b]
                    pool.wait_ge(work_free[bank], turn + 1)
                    if name in ("k", "q"):
                        pool.wait_ge(k_stored if name == "k" else q_stored, 32 * b)
                    pool.tensor_tensor(lo, whole[name][:], hi.bitcast(F32), ALU.subtract).then_inc(pool_parts[name], 1)
                    pool.wait_ge(pool_parts[name], pooled(name, b))
                if name == "weigh":
                    weigh(pool, b)
                    pool.wait_ge(weighed, 2 * b + 2)
                if name == "ctx":
                    wait_context(pool, b)
                    pool.wait_ge(c_ready, b)
                    link(pool.tensor_scalar(cT_hi[:, b % 2], cT[:, b % 2], 1.0, None, ALU.mult))
                    pool.tensor_tensor(cT_lo[:, b % 2], cT[:, b % 2], cT_hi[:, b % 2].bitcast(F32), ALU.subtract)\
                        .then_inc(c_ready, 1)
                    pool.wait_ge(c_ready, b + 1)
                if name == "minus":
                    own_rows()
                if name == "zeros":
                    zero_stack(b)
                if name == "ones":
                    for n in range(3):
                        pool.memset(vaug[:, n, :, :, HD:QUAD], 1.0).then_inc(vones, 1)
                    pool.wait_ge(vones, 3)
                if name == "consts":
                    other_constants()
                if name == "xo":
                    pool.wait_ge(bias_ready, 1)
                    if b >= 2:
                        pool.wait_ge(moments[1], b - 1)
                    for t in range(ST):
                        pool.tensor_tensor(xo[:, b % 2, t], xs[:, b, t], bo_sb[:], ALU.add).then_inc(xo_ready, 1)
                    pool.wait_ge(xo_ready, ST * (b + 1))

        @block.scalar
        def _(act):
            act.dma_start(cT[:, 0], ctxT[0].rearrange("(k p) t -> p k t", p=P)).then_inc(c_in[0], 16)
            act.dma_start(bk_sb[:], bk).then_inc(bias_in, 16)
            act.dma_start(bq_sb[:], bq).then_inc(bias_in, 16)
            for name, b, i in plan("scalar"):
                if (name, b) in WORK:
                    bank, turn = WORK[name, b]
                if name in WEIGHTS:
                    n, at = WEIGHTS[name]
                    act.wait_ge((wk_in, wq_in, wv_in)[n], 16)
                    act.copy(wa_hi[:, :, at], wa[:, :, at]).then_inc(wa_hi_ready, 1)
                if name == "qload":
                    query_stack(act, b, i)
                if name == "wf":
                    act.wait_ge(wf_in, 16)
                    act.copy(wf_hi[:], wf).then_inc(wf_hi_ready, 1)
                if name in ("xT", "x2T"):
                    w = int(name == "x2T")
                    act.wait_ge(work_ready[bank], turn + 1)
                    if (name, b) in ON_POOL:
                        if pooled(name, b) > 1:
                            act.wait_ge(pool_parts[name], pooled(name, b) - 1)
                    act.copy(xT_hi[:, w], work[bank][:]).then_inc(hi_ready[w], 1)
                    if (name, b) in ON_POOL:
                        act.copy(whole[name][:], work[bank][:]).then_inc(work_free[bank], 1)
                if name in ("k", "q"):
                    dst, bias, done, kept = (k_hi, bk_sb, khi_ready, k_stored) if name == "k" else (q_hi, bq_sb, qhi_ready, q_stored)
                    act.wait_ge(work_ready[bank], turn + 1)
                    act.wait_ge(bias_in, 32)
                    if b:
                        act.wait_ge(kept, 32 * b)
                    if pooled(name, b) > 1:
                        act.wait_ge(pool_parts[name], pooled(name, b) - 1)
                    for o in range(KT):
                        ins = act.activation(dst[:, o], work[bank][:, o], ACT.Identity, bias=bias[:, o:o + 1])
                    ins.then_inc(done, 1)
                    if (name, b) in ON_POOL:
                        for o in range(KT):
                            ins = act.activation(whole[name][:, o], work[bank][:, o], ACT.Identity, bias=bias[:, o:o + 1])
                        ins.then_inc(work_free[bank], 1)
                if name == "v":
                    act.wait_ge(work_ready[bank], turn + 1)
                    if b >= 3:
                        act.wait_ge(pv_done, GROUPS * (b - 2))
                    act.copy(vaug[:, b % 3, :, :, 0:HD], work[bank][:].rearrange("p t (h d) -> p t h d", d=HD))\
                        .then_inc(work_free[bank], 1)
                if name == "mrow":
                    act.wait_ge(work_ready[bank], turn + 1)
                    act.copy(qstack[b % NSTACK][ROWS:MROW, 0:2], work[bank][0:HEADS, 0:1].to_broadcast([HEADS, 2, S])).then_inc(work_free[bank], 1)
                if name == "attn":
                    n = HEADS * b + i
                    act.wait_ge(t_ready, n + 1)
                    if n == 0:
                        act.wait_ge(wa_lo_ready, 3)
                        act.wait_ge(wf_ready, 1)
                    if n >= NPROB:
                        act.wait_ge(pv_done, (n - NPROB) // 4 + 1)
                    act.activation(probs[:, n % NPROB], t_bank[n % 2][:], ACT.Exp, scale=SCALE).then_inc(exp_done, 1)
                if name == "low":
                    act.wait_ge(work_ready[bank], turn + 1)
                    if b:
                        act.wait_ge(weighed, 2 * b)
                    act.copy(low[:], work[bank][:, :, D - ER - E:D]).then_inc(work_free[bank], 1)
                if name == "exps":
                    act.wait_ge(below_ready, b + 1)
                    act.activation(ex[:], below[:], ACT.Exp).then_inc(e_ready, 1)
                if name in ("glu0", "glu1"):
                    act.wait_ge(work_ready[bank], turn + 1)
                    act.activation(th[:, int(name[3])], work[bank][:, 0], ACT.Tanh, scale=0.5).then_inc(th_ready, 1)
                if name in ("hT", "lT"):
                    act.wait_ge(work_ready[bank], turn + 1)
                    if b:
                        db, dt = WORK["down", b - 1]
                        act.wait_ge(work_ready[db], dt + 1)
                    if name == "hT":
                        act.copy(hidT[:], work[bank][:]).then_inc(work_free[bank], 1)
                    else:
                        act.copy(lT[:], work[bank][:, 0]).then_inc(work_free[bank], 1)

        @block.vector
        def _(dve):
            chain = [0]

            def link(ins):
                chain[0] += 1
                ins.then_inc(dve_chain, 1)
                dve.wait_ge(dve_chain, chain[0])

            dve.memset(kstack[0][:, 0:HEADS // 2].bitcast(F32), 0.0).then_inc(khalf, 1)

            def moments_of(src, w, b):
                for t in range(ST):
                    ins = dve.bn_stats(stats[:, w, b, t], src[:, t])
                link(ins)
                for t in range(ST):
                    ins = dve.bn_aggr(mv[:, w, b, t], stats[:, w, b, t])
                ins.then_inc(moments[w], 1)

            def wide(t):
                return t.unsqueeze(2).to_broadcast([P, ST, E])

            for name, b, i in plan("vector"):
                if (name, b) in WORK:
                    bank, turn = WORK[name, b]
                if name == "ctx":
                    wait_context(dve, b)
                    link(dve.tensor_copy(cT_hi[:, b % 2], cT[:, b % 2]))
                    dve.tensor_tensor(cT_lo[:, b % 2], cT[:, b % 2], cT_hi[:, b % 2].bitcast(F32), ALU.subtract)\
                        .then_inc(c_ready, 1)
                if name == "ln1":
                    dve.wait_ge(x_in[b], 16)
                    moments_of(xs[:, b], 0, b)
                if name in WEIGHTS:
                    n, at = WEIGHTS[name]
                    dve.wait_ge(wa_hi_ready, n + 1)
                    dve.tensor_tensor(wa_lo[:, :, at], wa[:, :, at], wa_hi[:, :, at].bitcast(F32),
                                      ALU.subtract).then_inc(wa_lo_ready, 1)
                if name in ("norm1", "norm2"):
                    w = int(name == "norm2")
                    src = x2[:, b] if w else xs[:, b]
                    dve.wait_ge(rstd_ready[w], b + 1)
                    if b:
                        tb, tt = WORK["x2T" if w else "xT", b - 1]
                        dve.wait_ge(work_ready[tb], tt + 1)
                    for t in range(ST):
                        ins = dve.tensor_scalar(xn[:, w, t], src[:, t], mv[:, w, b, t, 0:1], rstd[:, w, b, t:t + 1],
                                                ALU.subtract, ALU.mult)
                    ins.then_inc(xn_ready[w], 1)
                if name in ("xT", "x2T"):
                    w = int(name == "x2T")
                    dve.wait_ge(hi_ready[w], b + 1)
                    dve.tensor_tensor(xT_lo[:, w], work[bank][:], xT_hi[:, w].bitcast(F32), ALU.subtract)\
                        .then_inc(work_free[bank], 1)
                if name in ("k", "q"):
                    hi, lo, bias, up, kept = (k_hi, k_lo, bk_sb, khi_ready, k_stored) if name == "k" else \
                        (q_hi, q_lo, bq_sb, qhi_ready, q_stored)
                    if b:
                        dve.wait_ge(kept, 32 * b)
                    dve.wait_ge(up, b + 1)
                    for o in range(KT):
                        ins = dve.scalar_tensor_tensor(out=lo[:, o], in0=work[bank][:, o], scalar=bias[:, o:o + 1],
                                                       in1=hi[:, o].bitcast(F32), op0=ALU.add, op1=ALU.subtract)
                    ins.then_inc(work_free[bank], 1)
                if name == "bias":
                    dve.wait_ge(bias_product, 1)
                    dve.wait_ge(value_bias_in, 32)
                    dve.tensor_tensor(bo_sb[:], u_bank[:, 0], bo_sb[:], ALU.add).then_inc(bias_ready, 1)
                if name == "max":
                    n = HEADS * b + i
                    dve.wait_ge(s_ready, n + 1)
                    dve.tensor_reduce(rowmax[:, b % 2, :, i], s_bank[n % 2][:], AX.X, ALU.max).then_inc(max_done, 1)
                if name == "pv":
                    n = GROUPS * b + i
                    dve.wait_ge(pv_done, n + 1)
                    dve.transpose(uT[:, i], u_bank[:, 0]).then_inc(u_read, 1)
                    dve.wait_ge(u_read, n + 1)
                    link(dve.reciprocal(rden[:, i], uT[:, i, :, HD]))
                    ins = dve.tensor_tensor(un[:, i // 2, :, i % 2], uT[:, i, :, 0:HD],
                                            rden[:, i].unsqueeze(2).to_broadcast([P, BLK, HD]), ALU.mult)
                    if i % 2:
                        link(ins)
                        if b and i == 1:
                            ob, ot = WORK["o", b - 1]
                            dve.wait_ge(work_ready[ob], ot + 1)
                        dve.transpose(attnT[:, i // 2], un[:, i // 2]).then_inc(attn_ready, 1)
                if name == "o":
                    dve.wait_ge(work_ready[bank], turn + 1)
                    dve.wait_ge(xo_ready, ST * (b + 1))
                    ins = dve.tensor_tensor(x2[:, b], work[bank][:], xo[:, b % 2], ALU.add)
                    ins.then_inc(work_free[bank], 1)
                if name == "ln2":
                    ob, ot = WORK["o", b]
                    dve.wait_ge(work_free[ob], ot + 1)
                    moments_of(x2[:, b], 1, b)
                if name == "route1":
                    lb_, lt = WORK["low", b]
                    dve.wait_ge(work_free[lb_], lt + 1)
                    logit = low[:, :, ER:ER + E]
                    link(dve.tensor_reduce(top[:], logit, AX.X, ALU.max))
                    dve.tensor_tensor(below[:], logit, wide(top[:]), ALU.subtract).then_inc(below_ready, 1)
                    dve.wait_ge(below_ready, b + 1)
                if name == "route2":
                    if b == 0:
                        dve.wait_ge(earlier_ready, 1)
                    own = below[:].unsqueeze(3).to_broadcast([P, ST, E, E])
                    other = below[:].unsqueeze(2).to_broadcast([P, ST, E, E])
                    dve.tensor_tensor(tied[:], other, own, ALU.is_equal).then_inc(dve_chain, 1)
                    chain[0] += 1
                    dve.tensor_tensor(ahead[:], other, own, ALU.is_gt).then_inc(dve_chain, 1)
                    dve.wait_ge(dve_chain, chain[0])
                    chain[0] += 1
                    link(dve.tensor_tensor(tied[:], tied[:], earlier[:].unsqueeze(1).to_broadcast([P, ST, E, E]), ALU.mult))
                    link(dve.tensor_tensor(ahead[:], ahead[:], tied[:], ALU.add))
                if name == "route3":
                    link(dve.tensor_reduce(rank[:], ahead[:], AX.X, ALU.add))
                    dve.wait_ge(e_ready, b + 1)
                    link(dve.tensor_reduce(esum[:], ex[:], AX.X, ALU.add))
                    dve.reciprocal(einv[:], esum[:]).then_inc(dve_chain, 1)
                    chain[0] += 1
                    link(dve.scalar_tensor_tensor(out=ex[:], in0=rank[:], scalar=1.5, in1=ex[:], op0=ALU.is_lt,
                                                  op1=ALU.mult))
                    dve.tensor_tensor(wexp[:], ex[:], wide(einv[:]), ALU.mult).then_inc(weights_ready, 1)
                if name in ("glu0", "glu1"):
                    t = int(name[3])
                    dve.wait_ge(th_ready, ST * b + t + 1)
                    if b and t == 0:
                        tb, tt = WORK["hT", b - 1]
                        dve.wait_ge(work_ready[tb], tt + 1)
                    link(dve.scalar_tensor_tensor(out=hid[:, t], in0=th[:, t], scalar=1.0, in1=work[bank][:, 0],
                                                  op0=ALU.add, op1=ALU.mult))
                    dve.scalar_tensor_tensor(out=hid[:, t], in0=work[bank][:, 1], scalar=0.5, in1=hid[:, t],
                                             op0=ALU.mult, op1=ALU.mult).then_inc(work_free[bank], 1)
                if name == "weigh":
                    weigh(dve, b)
                if name == "down":
                    dve.wait_ge(work_ready[bank], turn + 1)
                    if b >= 2:
                        dve.wait_ge(stored[b - 2], 16)
                    dve.tensor_tensor(res[:, b % 2], work[bank][:], x2[:, b], ALU.add).then_inc(work_free[bank], 1)

        @block.tensor
        def _(pe):
            def product(dst, left, right, terms=((0, 0), (0, 1), (1, 0))):
                steps = [(k, i, j) for i, j in terms for k in range(KT)]
                for n, (k, i, j) in enumerate(steps):
                    ins = pe.matmul(dst, left(i, k), right(j, k), start=(n == 0), stop=(n == len(steps) - 1))
                return ins

            def keep_warm(n):
                for _ in range(n):
                    pe.matmul(t_bank[0][:, 0, 0:P], ident[:], ident[:], start=True, stop=True)

            wap, wfp, cp = (wa_hi, wa_lo), (wf_hi, wf_lo), (cT_hi, cT_lo)
            xp = (xT_hi, xT_lo)
            pe.wait_ge(consts, 2)
            for name, b, i in plan("tensor"):
                if (name, b) in WORK:
                    bank, turn = WORK[name, b]
                    dst = work[bank]
                    if turn:
                        pe.wait_ge(work_free[bank], turn)
                if name in ("xT", "x2T"):
                    w = int(name == "x2T")
                    pe.wait_ge(xn_ready[w], b + 1)
                    for k in range(KT):
                        for t in range(ST):
                            ins = pe.transpose(dst[:, k, t * P:(t + 1) * P], xn[:, w, t, k * P:(k + 1) * P], ident[:])
                    ins.then_inc(work_ready[bank], 1)
                if name == "k":
                    pe.wait_ge(wa_lo_ready, 1)
                    pe.wait_ge(c_ready, b + 1)
                    for o in range(KT):
                        ins = product(dst[:, o], lambda i, k: wap[i][:, k, o * P:(o + 1) * P], lambda j, k: cp[j][:, b % 2, k])
                    ins.then_inc(work_ready[bank], 1)
                if name == "q":
                    pe.wait_ge(wa_lo_ready, 2)
                    wait_parts(pe, "xT", b)
                    for o in range(KT):
                        ins = product(dst[:, o], lambda i, k: wap[i][:, k, D + o * P:D + (o + 1) * P],
                                      lambda j, k: xp[j][:, 0, k])
                    ins.then_inc(work_ready[bank], 1)
                if name == "v":
                    pe.wait_ge(wa_lo_ready, 3)
                    pe.wait_ge(c_ready, b + 1)
                    for t in range(TT):
                        ins = product(dst[:, t], lambda i, k: cp[i][:, b % 2, k, t * P:(t + 1) * P],
                                      lambda j, k: wap[j][:, k, 2 * D:3 * D])
                    ins.then_inc(work_ready[bank], 1)
                if name == "bias":
                    pe.wait_ge(wo_in, 16)
                    pe.wait_ge(value_bias_in, 32)
                    for k in range(KT):
                        ins = pe.matmul(u_bank[:, 0], bv_sb[:, k:k + 1].to_broadcast([P, P]), wo[:, k],
                                        start=(k == 0), stop=(k == KT - 1))
                    ins.then_inc(bias_product, 1)
                if name == "max":
                    n = HEADS * b + i
                    if b + i == 0:
                        keep_warm(NWARM)
                    if i == 0:
                        pe.wait_ge(k_stacked[b % NSTACK], 96 * (b // NSTACK + 1))
                        pe.wait_ge(q_stacked[b % NSTACK], 48 * (b // NSTACK + 1))
                    if b == 0 and i == HEADS // 2:
                        pe.wait_ge(q_late, 48)
                    if n >= 2:
                        pe.wait_ge(max_done, n - 1)
                    ks, qs = kstack[b % NSTACK], qstack[b % NSTACK]
                    for t in range(ST):
                        ins = pe.matmul(s_bank[n % 2][:, t], qs[0:ROWS, i // 2, t * P:(t + 1) * P], ks[0:ROWS, i],
                                        start=True, stop=True)
                    ins.then_inc(s_ready, 1)
                if name == "mrow":
                    pe.wait_ge(max_done, HEADS * (b + 1))
                    for t in range(ST):
                        ins = pe.transpose(dst[0:HEADS, 0, t * P:(t + 1) * P], rowmax[:, b % 2, t], ident[:])
                    ins.then_inc(work_ready[bank], 1)
                if name == "attn":
                    n = HEADS * b + i
                    if n >= 2:
                        pe.wait_ge(exp_done, n - 1)
                    if i == 0:
                        mb, mt = WORK["mrow", b]
                        pe.wait_ge(work_free[mb], mt + 1)
                        if b < NSTACK:
                            pe.wait_ge(kminus[b], 16 if b else 1)
                    elif i == 4:
                        pe.wait_ge(mrow_ready[b], 16)
                    ks, qs = kstack[b % NSTACK], qstack[b % NSTACK]
                    for t in range(TT):
                        ins = pe.matmul(t_bank[n % 2][:, t], ks[0:MROW, i, t * P:(t + 1) * P], qs[0:MROW, i // 2],
                                        start=True, stop=True)
                    ins.then_inc(t_ready, 1)
                if name == "pv":
                    n = GROUPS * b + i
                    pe.wait_ge(exp_done, HEADS * b + 4 * i + 4)
                    if n:
                        pe.wait_ge(u_read, n)
                    if i == 0:
                        vb, vt = WORK["v", b]
                        pe.wait_ge(work_free[vb], vt + 1)
                        pe.wait_ge(vones, 3)
                        pe.wait_ge(bias_ready, 1)
                    for t in range(TT):
                        for j in range(4):
                            h = 4 * i + j
                            ins = pe.matmul(u_bank[QUAD * j:QUAD * (j + 1), 0], vaug[:, b % 3, t, h],
                                            probs[:, (HEADS * b + h) % NPROB, t], start=(t == 0), stop=(t == TT - 1),
                                            tile_position=(0, QUAD * j))
                    ins.then_inc(pv_done, 1)
                if name == "o":
                    pe.wait_ge(wo_in, 16)
                    pe.wait_ge(attn_ready, 2 * (b + 1))
                    for t in range(ST):
                        for k in range(2):
                            ins = pe.matmul(dst[:, t], attnT[:, k, t * P:(t + 1) * P], wo[:, k], start=(k == 0),
                                            stop=(k == 1))
                    ins.then_inc(work_ready[bank], 1)
                if name in ("low", "glu0", "glu1"):
                    if name == "low":
                        pe.wait_ge(wf_ready, 1)
                        wait_parts(pe, "x2T", b)
                        for t in range(ST):
                            ins = product(dst[:, t], lambda i, k: xp[i][:, 1, k, t * P:(t + 1) * P],
                                          lambda j, k: wfp[j][:, k, WF - D:WF])
                    else:
                        t = int(name[3])
                        ins = product(dst[:].rearrange("p o f -> p (o f)"),
                                      lambda i, k: xp[i][:, 1, k, t * P:(t + 1) * P],
                                      lambda j, k: wfp[j][:, k, 0:2 * EF])
                    ins.then_inc(work_ready[bank], 1)
                if name == "hT":
                    pe.wait_ge(weighed, 2 * b + 1)
                    for k in range(EF // P):
                        for t in range(ST):
                            ins = pe.transpose(dst[:, k, t * P:(t + 1) * P], hid[:, t, k * P:(k + 1) * P], ident[:])
                    ins.then_inc(work_ready[bank], 1)
                if name == "lT":
                    pe.wait_ge(weighed, 2 * b + 2)
                    for t in range(ST):
                        ins = pe.transpose(dst[:, 0, t * P:(t + 1) * P], lw[:, t], ident[:])
                    ins.then_inc(work_ready[bank], 1)
                if name == "down":
                    if b == 0:
                        pe.wait_ge(wd_in, 32)
                    for st in ("hT", "lT"):
                        sb_, s_t = WORK[st, b]
                        pe.wait_ge(work_free[sb_], s_t + 1)
                    for t in range(ST):
                        at = slice(t * P, (t + 1) * P)
                        pe.matmul(dst[:, t], hidT[:, 0, at], wd[:, 0], start=True, stop=False)
                        pe.matmul(dst[:, t], hidT[:, 1, at], wd[:, 1], start=False, stop=False)
                        ins = pe.matmul(dst[:, t], lT[:, at], lb[:], start=False, stop=True)
                    ins.then_inc(work_ready[bank], 1)


def kernel(**inputs):
    import numpy as np
    import concourse.bacc as bacc
    from concourse.bass_utils import run_bass_kernel_spmd as run

    a = {k: np.asarray(v) for k, v in inputs.items()}
    flat = lambda w: w.reshape(-1, w.shape[-1]).T
    wo = a["L0_xattn_Wo"].T.reshape(2, 2, 4, HD, D).transpose(2, 1, 3, 0, 4)
    arrays = {
        "x": a["x"],
        "ctxT": a["ctx_2048"].transpose(0, 2, 1),
        "wattn": np.concatenate([a["L0_xattn_Wk"].T, a["L0_xattn_Wq"].T, a["L0_xattn_Wv"].T], 1),
        "wffn": np.concatenate([flat(a["L0_ffn_gate_w"]), flat(a["L0_ffn_up_w"]), flat(a["L0_ffn_lora_A"]),
                                a["L0_ffn_G"]], 1),
        "woT": wo.reshape(P, 2, D),
        "wdown": a["L0_ffn_down_w"].transpose(0, 2, 1).reshape(EF, D),
        "loraB": a["L0_ffn_lora_B"].transpose(0, 2, 1).reshape(ER, D),
        "bq": a["L0_xattn_bq"].reshape(KT, P).T, "bk": a["L0_xattn_bk"].reshape(KT, P).T,
        "bv": a["L0_xattn_bv"].reshape(2, 2, 4, HD).transpose(2, 1, 3, 0).reshape(P, 2), "bo": a["L0_xattn_bo"],
    }
    nc = bacc.Bacc("TRN2", target_bir_lowering=False, num_devices=1)
    args = []
    for name, v in arrays.items():
        arrays[name] = v = np.ascontiguousarray(v)
        args.append(nc.dram_tensor(name, v.shape, mybir.dt.from_np(v.dtype), kind="ExternalInput").ap())
    args.append(nc.dram_tensor("out", [B, S, D], F32, kind="ExternalOutput").ap())
    xattn_moe_kernel(nc, *args)
    r = run(nc, [arrays], core_ids=[0])
    return r.results[0]["out"]
```
